# Optimizing a Trainium2 kernel written in Bass

```python
import numpy as np
import jax
import jax.numpy as jnp

def _softmax(x, axis=-1):
    return jax.nn.softmax(x, axis=axis)

def _gelu(x):
    return jax.nn.gelu(x, approximate=True)

def _silu(x):
    return jax.nn.silu(x)

def _sigmoid(x):
    return jax.nn.sigmoid(x)

def _layernorm(x, axis=-1, eps=1e-05):
    m = jnp.mean(x, axis=axis, keepdims=True)
    v = jnp.var(x, axis=axis, keepdims=True)
    return (x - m) / jnp.sqrt(v + eps)

def _scatter_add(tgt, idx, src, axis=0):
    return tgt.at[idx].add(src)

def _segment_sum(src, seg, n):
    return jax.ops.segment_sum(src, seg, n)
kernel_name = 'mk_decoder_postln_d1_seqx_r2_44c2c3'

def setup_inputs(seed: int=0):
    np.random.seed(seed)
    _w = jnp.asarray

    def _rec_inputs():
        import jax
        import jax.numpy as jnp
        _rk = jax.random.key(seed)
        x = -0.0002928 + 1 * jax.random.normal(jax.random.fold_in(_rk, 1), (2, 1024, 512), jnp.float32)
        _lenS = 1024 - jax.random.randint(jax.random.fold_in(_rk, 7), (2,), 0, max(1, 1024 // 4) + 1, jnp.int32)
        _lenS2 = 2048 - jax.random.randint(jax.random.fold_in(_rk, 8), (2,), 0, max(1, 2048 // 4) + 1, jnp.int32)
        _ctx_1024P = jax.random.normal(jax.random.fold_in(_rk, 11), (2, 16, 512), jnp.float32)
        _ctx_1024c = jax.random.dirichlet(jax.random.fold_in(_rk, 511), 0.3 * jnp.ones((16,), jnp.float32), (2, 2048))
        _ctx_1024t = jnp.einsum('bsk,bkd->bsd', _ctx_1024c, _ctx_1024P)
        _ctx_1024t = _ctx_1024t * jax.lax.rsqrt(jnp.mean(jnp.square(_ctx_1024t)) + 1e-12) * 0.953939
        ctx_1024 = -1.39393e-06 + 0.999914 * (_ctx_1024t + 0.3 * jax.random.normal(jax.random.fold_in(_rk, 611), (2, 2048, 512), jnp.float32))
        return (x, ctx_1024)
    x, ctx_1024 = _rec_inputs()

    def _L0_attn_setup():
        import jax, jax.numpy as jnp
        import numpy as np
        B, T, C = (4, 2048, 512)
        H = 16
        D = C // H
        W_SCALE = 0.02
        key = jax.random.key(seed)
        ks = jax.random.split(key, 9)
        inp = {'x': jax.random.normal(ks[0], (B, T, C), dtype=jnp.float32)}
        for i, nm in enumerate(['q', 'k', 'v', 'o']):
            inp[f'W{nm}'] = jax.random.normal(ks[1 + i], (C, C), dtype=jnp.float32) * W_SCALE
            inp[f'b{nm}'] = jnp.zeros((C,), dtype=jnp.float32)
        return inp
    _L0_attn_all = _L0_attn_setup()
    _L0_attn_in = {k: v for k, v in _L0_attn_all.items() if k in ('Wq', 'bq', 'Wk', 'bk', 'Wv', 'bv', 'Wo', 'bo')}
    del _L0_attn_all

    def _L0_xattn_setup():
        import jax, jax.numpy as jnp
        import numpy as np
        DIM = 512
        HEADS = 16
        HEAD_DIM = DIM // HEADS
        SCALE = HEAD_DIM ** (-0.5)
        key = jax.random.key(seed)
        ks = jax.random.split(key, 7)
        b, n = (2, 1024)
        x1 = jax.random.normal(ks[0], (b, n, DIM), dtype=jnp.float32)
        x2 = jax.random.normal(ks[1], (b, n, DIM), dtype=jnp.float32)
        s = DIM ** (-0.5)
        wq = jax.random.normal(ks[2], (DIM, DIM), dtype=jnp.float32) * s
        wk = jax.random.normal(ks[3], (DIM, DIM), dtype=jnp.float32) * s
        wv = jax.random.normal(ks[4], (DIM, DIM), dtype=jnp.float32) * s
        wo = jax.random.normal(ks[5], (DIM, DIM), dtype=jnp.float32) * s
        bo = jax.random.normal(ks[6], (DIM,), dtype=jnp.float32) * 0.01
        return {'x1': x1, 'x2': x2, 'wq': wq, 'wk': wk, 'wv': wv, 'wo': wo, 'bo': bo}
    _L0_xattn_all = _L0_xattn_setup()
    _L0_xattn_in = {k: v for k, v in _L0_xattn_all.items() if k in ('wq', 'wk', 'wv', 'wo', 'bo')}
    del _L0_xattn_all

    def _L0_ffn_setup():
        import math
        import jax, jax.numpy as jnp
        import numpy as np
        E = 8
        K = 2
        CF = 1.25
        D = 512
        F = 1024
        B, S = (4, 1024)
        key = jax.random.key(seed)
        ks = jax.random.split(key, 8)
        sd = 1.0 / math.sqrt(D)
        sf = 1.0 / math.sqrt(F)
        return {'x': jax.random.normal(ks[0], (B, S, D), jnp.float32), 'router_w': jax.random.normal(ks[1], (D, E), jnp.float32) * sd, 'router_b': jnp.zeros((E,), jnp.float32), 'w1': jax.random.normal(ks[2], (E, D, F), jnp.float32) * sd, 'b1': jax.random.normal(ks[3], (E, F), jnp.float32) * 0.01, 'w2': jax.random.normal(ks[4], (E, F, D), jnp.float32) * sf, 'b2': jax.random.normal(ks[5], (E, D), jnp.float32) * 0.01}
    _L0_ffn_all = _L0_ffn_setup()
    _L0_ffn_in = {k: v for k, v in _L0_ffn_all.items() if k in ('router_w', 'router_b', 'w1', 'b1', 'w2', 'b2')}
    del _L0_ffn_all
    return {'x': x, 'ctx_1024': ctx_1024, 'L0_attn_Wq': _L0_attn_in['Wq'], 'L0_attn_bq': _L0_attn_in['bq'], 'L0_attn_Wk': _L0_attn_in['Wk'], 'L0_attn_bk': _L0_attn_in['bk'], 'L0_attn_Wv': _L0_attn_in['Wv'], 'L0_attn_bv': _L0_attn_in['bv'], 'L0_attn_Wo': _L0_attn_in['Wo'], 'L0_attn_bo': _L0_attn_in['bo'], 'L0_xattn_wq': _L0_xattn_in['wq'], 'L0_xattn_wk': _L0_xattn_in['wk'], 'L0_xattn_wv': _L0_xattn_in['wv'], 'L0_xattn_wo': _L0_xattn_in['wo'], 'L0_xattn_bo': _L0_xattn_in['bo'], 'L0_ffn_router_w': _L0_ffn_in['router_w'], 'L0_ffn_router_b': _L0_ffn_in['router_b'], 'L0_ffn_w1': _L0_ffn_in['w1'], 'L0_ffn_b1': _L0_ffn_in['b1'], 'L0_ffn_w2': _L0_ffn_in['w2'], 'L0_ffn_b2': _L0_ffn_in['b2']}

def reference(x, ctx_1024, L0_attn_Wq, L0_attn_bq, L0_attn_Wk, L0_attn_bk, L0_attn_Wv, L0_attn_bv, L0_attn_Wo, L0_attn_bo, L0_xattn_wq, L0_xattn_wk, L0_xattn_wv, L0_xattn_wo, L0_xattn_bo, L0_ffn_router_w, L0_ffn_router_b, L0_ffn_w1, L0_ffn_b1, L0_ffn_w2, L0_ffn_b2):
    import jax
    import jax.numpy as jnp

    def _L0_attn_ref(x, Wq, bq, Wk, bk, Wv, bv, Wo, bo):
        import jax, jax.numpy as jnp
        import numpy as np
        B, T, C = (4, 2048, 512)
        H = 16
        D = C // H
        W_SCALE = 0.02
        Bx, Tx, Cx = x.shape
        q = (x @ Wq.T + bq).reshape(Bx, Tx, H, D)
        k = (x @ Wk.T + bk).reshape(Bx, Tx, H, D)
        v = (x @ Wv.T + bv).reshape(Bx, Tx, H, D)
        q = jax.nn.elu(q) + 1.0
        k = jax.nn.elu(k) + 1.0
        kv = jnp.einsum('bthd,bthe->bhde', k, v)
        denom = jnp.einsum('bthd,bhd->bth', q, k.sum(axis=1))
        num = jnp.einsum('bthd,bhde->bthe', q, kv)
        out = num / jnp.clip(denom, 1e-06, None)[..., None]
        out = out.reshape(Bx, Tx, Cx)
        return out @ Wo.T + bo

    def _L0_xattn_ref(x1, x2, wq, wk, wv, wo, bo):
        import jax, jax.numpy as jnp
        import numpy as np
        DIM = 512
        HEADS = 16
        HEAD_DIM = DIM // HEADS
        SCALE = HEAD_DIM ** (-0.5)
        b, n, _ = x1.shape
        m = x2.shape[1]
        q = (x1 @ wq.T).reshape(b, n, HEADS, HEAD_DIM).transpose(0, 2, 1, 3)
        k = (x2 @ wk.T).reshape(b, m, HEADS, HEAD_DIM).transpose(0, 2, 1, 3)
        v = (x2 @ wv.T).reshape(b, m, HEADS, HEAD_DIM).transpose(0, 2, 1, 3)
        dots = jnp.einsum('bhnd,bhmd->bhnm', q, k) * SCALE
        attn = jax.nn.softmax(dots, axis=-1)
        out = jnp.einsum('bhnm,bhmd->bhnd', attn, v)
        out = out.transpose(0, 2, 1, 3).reshape(b, n, DIM)
        return out @ wo.T + bo

    def _L0_ffn_ref(x, router_w, router_b, w1, b1, w2, b2):
        import math
        import jax, jax.numpy as jnp
        import numpy as np
        E = 8
        K = 2
        CF = 1.25
        D = 512
        F = 1024
        B, S = (4, 1024)
        b, s, d = x.shape
        xf = x.reshape(-1, d)
        T = b * s
        A = T * K
        cap = max(1, int(math.ceil(CF * A / E)))
        logits = xf @ router_w + router_b
        probs = jax.nn.softmax(logits, axis=-1)
        topk_p, topk_i = jax.lax.top_k(probs, K)
        topk_p = topk_p / jnp.clip(topk_p.sum(-1, keepdims=True), 1e-09)
        a_tok = jnp.repeat(jnp.arange(T), K)
        a_exp = topk_i.reshape(-1)
        a_w = topk_p.reshape(-1)
        order = jnp.argsort(a_exp)
        se, st, sw = (a_exp[order], a_tok[order], a_w[order])
        counts = jnp.bincount(se, length=E)
        starts = jnp.cumsum(counts) - counts
        rank = jnp.arange(A) - starts[se]
        keep = rank < cap
        slot = jnp.where(keep, se * cap + rank, E * cap)
        buf = jnp.zeros((E * cap + 1, d), x.dtype).at[slot].set(xf[st])
        buf = buf[:-1].reshape(E, cap, d)
        h = jax.nn.gelu(jnp.einsum('ecd,edf->ecf', buf, w1) + b1[:, None, :], approximate=False)
        eo = jnp.einsum('ecf,efd->ecd', h, w2) + b2[:, None, :]
        eo_flat = jnp.concatenate([eo.reshape(E * cap, d), jnp.zeros((1, d), x.dtype)], axis=0)
        w = jnp.where(keep, sw, 0.0)[:, None]
        out = jnp.zeros_like(xf).at[st].add(eo_flat[slot] * w)
        return out.reshape(b, s, d)
    x = _layernorm(x + _L0_attn_ref(x, L0_attn_Wq, L0_attn_bq, L0_attn_Wk, L0_attn_bk, L0_attn_Wv, L0_attn_bv, L0_attn_Wo, L0_attn_bo), axis=-1)
    x = _layernorm(x + _L0_xattn_ref(x, ctx_1024, L0_xattn_wq, L0_xattn_wk, L0_xattn_wv, L0_xattn_wo, L0_xattn_bo), axis=-1)
    x = _layernorm(x + _L0_ffn_ref(x, L0_ffn_router_w, L0_ffn_router_b, L0_ffn_w1, L0_ffn_b1, L0_ffn_w2, L0_ffn_b2), axis=-1)
    return x

_drawn_inputs = setup_inputs


def setup_inputs(seed=0):
    import zlib

    import numpy as np

    out = dict(_drawn_inputs(seed))
    spreads = {'L0_attn_bq': (0.0, 0.8),
     'L0_attn_bk': (0.0, 0.8),
     'L0_attn_bv': (0.0, 0.1),
     'L0_attn_bo': (0.0, 0.1),
     'L0_ffn_router_b': (0.0, 0.1)}
    factors = {'L0_attn_Wq': 8.0, 'L0_attn_Wk': 5.138, 'L0_ffn_b1': 8.0, 'L0_ffn_b2': 8.0}
    for name, (base, spread) in spreads.items():
        noise = np.random.default_rng([zlib.crc32(name.encode()), seed]).standard_normal(out[name].shape)
        drawn = base * np.exp(spread * noise) if base else spread * noise
        out[name] = jnp.asarray(drawn.astype(out[name].dtype))
    for name, factor in factors.items():
        out[name] = (out[name] * factor).astype(out[name].dtype)
    return out
```

```python
import numpy as np
from contextlib import ExitStack

import concourse.bass as bass
from concourse import mybir

F32 = mybir.dt.float32
F32R = mybir.dt.float32r
I32 = mybir.dt.int32
U32 = mybir.dt.uint32
ALU = mybir.AluOpType
ACT = mybir.ActivationFunctionType
AX = mybir.AxisListType

P = 128
B, T, M, D = 2, 1024, 2048, 512
H, DH = 16, 32
HG = P // DH
NG = H // HG
NC = D // P
NT = T // P
NTOK = B * T
MT = M // P
HALF = 512
NH = T // HALF
E, F, TOPK = 8, 1024, 2
NF = F // P
CAP = -(-5 * NTOK * TOPK // (4 * E))
NS = CAP // P
SLOTS = E * CAP
SCALE = float(DH) ** -0.5
EPS = 1e-5
STK = 3 * DH
SHIFT = 2
RSQRT_MAGIC = 0x5F3759DF


class Engine:

    def __init__(self, handle, sem):
        self.handle, self.sem, self.count, self.queue, self.seen = handle, sem, 0, [], {}

    def wait(self, *tokens):
        for token in tokens:
            if token is None:
                continue
            sem, value = token
            if self.seen.get(id(sem), 0) < value:
                self.seen[id(sem)] = value
                self.queue.append((None, (sem, value), {}, None, 0))

    def quiet(self, fn, *args, **kw):
        self.queue.append((fn, args, kw, None, 0))

    def run(self, fn, *args, **kw):
        self.count += 1
        self.queue.append((fn, args, kw, self.sem, 1))
        return (self.sem, self.count)

    def then(self, fn, *args, **kw):
        if self.count:
            self.wait((self.sem, self.count))
        return self.run(fn, *args, **kw)

    def dma(self, stream, out, in_, **kw):
        stream.count += 16
        self.queue.append((self.handle.dma_start, (out, in_), kw, stream.sem, 16))
        return (stream.sem, stream.count)

    def indirect(self, stream, **kw):
        stream.count += 16
        self.queue.append((self.handle.indirect_dma_start, (), kw, stream.sem, 16))
        return (stream.sem, stream.count)

    def last(self):
        return (self.sem, self.count) if self.count else None

    def emit(self):
        for fn, args, kw, sem, by in self.queue:
            if fn is None:
                self.handle.wait_ge(*args)
            elif sem is None:
                fn(*args, **kw)
            else:
                fn(*args, **kw).then_inc(sem, by)


class Stream:

    def __init__(self, sem):
        self.sem, self.count = sem, 0

    def all(self):
        return (self.sem, self.count) if self.count else None


def program(nc, t):
    ctx = ExitStack()
    with ctx:
        def sem(name):
            return ctx.enter_context(nc.semaphore(name))

        pe = Engine(nc.tensor, sem("pe_done"))
        dve = Engine(nc.vector, sem("dve_done"))
        act = Engine(nc.scalar, sem("act_done"))
        pool = Engine(nc.gpsimd, sem("pool_done"))
        sp = Engine(nc.sync, sem("sp_done"))
        engines = [pe, dve, act, pool, sp]
        streams = []

        def stream(name):
            streams.append(Stream(sem(name)))
            return streams[-1]

        def streams_of(name, n):
            return [stream(f"{name}{i}") for i in range(n)]

        def sb(scope, name, shape, dt=F32):
            return scope.enter_context(nc.sbuf_tensor(name, shape, dt))

        V, S, G = nc.vector, nc.scalar, nc.gpsimd

        q_parts = nc.dram_tensor("q_parts", (B, H, 2, DH, T), F32).ap()
        k_parts = nc.dram_tensor("k_parts", (B, H, 2, DH, M), F32).ap()
        v_rows = nc.dram_tensor("v_rows", (B, NG, P, MT, P), F32).ap()
        x1_rows = nc.dram_tensor("x1_rows", (NTOK, D), F32).ap()
        x2_rows = nc.dram_tensor("x2_rows", (NTOK + P, D), F32).ap()
        y_rows = nc.dram_tensor("y_rows", (NTOK + P, D), F32).ap()
        slot_table = nc.dram_tensor("slot_table", (SLOTS + P, 2), I32).ap()

        pairs = [ctx.enter_context(nc.psum_tensor(f"banks{2 * i}", [P, 2, HALF], F32)) for i in range(4)]
        bank_free = [None] * 8

        def bank(i):
            return pairs[i // 2][:, i % 2, :]

        def accumulate(out, operands, start=True, stop=True):
            for n, (lhsT, rhs) in enumerate(operands):
                first, last = start and n == 0, stop and n == len(operands) - 1
                issue = pe.run if n == len(operands) - 1 else pe.quiet
                done = issue(nc.tensor.matmul, out, lhsT, rhs, start=first, stop=last)
            return done

        identity = sb(ctx, "identity", [P, P])
        same_head = sb(ctx, "same_head", [P, P])
        head_of = sb(ctx, "head_of", [P, HG])
        earlier = sb(ctx, "earlier", [P, P])
        ones = sb(ctx, "ones", [P, P])
        expert_no = sb(ctx, "expert_no", [P, E])
        expert_base = sb(ctx, "expert_base", [P, E])
        router_bias = sb(ctx, "router_bias", [P, E])
        router_w = sb(ctx, "router_w", [P, NC, E])
        token_id = sb(ctx, "token_id", [P, B * NT], I32)
        dump_slot = sb(ctx, "dump_slot", [P, 1])
        stats = sb(ctx, "stats", [P, 6])
        mean_var = sb(ctx, "mean_var", [P, NT, 2])
        rs_a, rs_b, rs_y = (sb(ctx, f"rsqrt_{n}", [P, NT]) for n in ("a", "b", "y"))
        const_in = stream("const_in")
        for tile, src in ((identity, t["identity"]), (same_head, t["same_head"]), (head_of, t["head_of"]),
                          (earlier, t["earlier"]), (ones, t["ones"]), (expert_no, t["expert_no"]),
                          (expert_base, t["expert_base"]), (token_id, t["token_id"]),
                          (dump_slot, t["dump_slot"])):
            pool.dma(const_in, tile[:, :], src)
        pool.dma(const_in, router_bias[:, :], t["L0_ffn_router_b"].partition_broadcast(P))
        pool.dma(const_in, router_w[:, :, :], t["L0_ffn_router_w"].rearrange("(c p) e -> p c e", p=P))
        scratch_init = stream("scratch_init")
        pool.dma(scratch_init, slot_table, t["table_init"])
        pool.dma(scratch_init, x2_rows[NTOK:, :], t["zeros"])
        pool.dma(scratch_init, y_rows[NTOK:, :], t["zeros"])

        def rsqrt_of_variances(n):
            var, a, b, y = mean_var[:, 0:n, 1], rs_a[:, 0:n], rs_b[:, 0:n], rs_y[:, 0:n]
            dve.then(V.tensor_scalar, a, var, EPS, None, ALU.add)
            dve.then(V.tensor_scalar, y.bitcast(I32), a.bitcast(I32), 1, None, ALU.logical_shift_right)
            dve.then(V.tensor_scalar, y.bitcast(I32), y.bitcast(I32), -1.0, float(RSQRT_MAGIC), ALU.mult, ALU.add)
            dve.then(V.tensor_scalar, a, a, -0.5, None, ALU.mult)
            for _ in range(4):
                dve.then(V.tensor_tensor, b, y, y, ALU.mult)
                dve.then(V.tensor_tensor, b, b, a, ALU.mult)
                done = dve.then(V.scalar_tensor_tensor, y, b, 1.5, y, ALU.add, ALU.mult)
            return done

        def tile_statistics(row, n):
            dve.then(V.bn_stats, stats[:, :], row)
            return dve.then(V.bn_aggr, mean_var[:, n, :], stats[:, :])

        def normalise(out, row, n):
            return dve.run(V.tensor_scalar, out, row, mean_var[:, n, 0:1], rs_y[:, n:n + 1],
                           ALU.subtract, ALU.mult)

        def join(*extra):
            ends = [x.last() for x in engines] + [s.all() for s in streams] + list(extra)
            for engine in engines:
                engine.wait(*ends)

        k_out, v_out, q_out = streams_of("k_out", 2), streams_of("v_out", 2), streams_of("q_out", 2)
        x1_out = stream("x1_out")
        pe.wait(const_in.all() or None)

        with ExitStack() as scope:
            weights = {}
            w_in = {}
            for name in ("k", "v", "q", "o", "xq"):
                weights[name] = sb(scope, f"w{name}_t", [P, NC, D])
                w_in[name] = stream(f"w{name}_in")
            x_t = [sb(scope, f"x_t{b}", [P, NC, T]) for b in range(B)]
            x_nat = sb(scope, "x_nat", [P, NT, D])
            bias_rows = {n: sb(scope, f"b{n}_row", [P, D]) for n in ("k", "v", "o")}
            bq_col = sb(scope, "bq_col", [P, NG])
            q_t = sb(scope, "q_t", [P, NG, T])
            k_nat = sb(scope, "k_nat", [P, NT, D])
            v_nat = sb(scope, "v_nat", [P, NT, NG, P + 1])
            kv = sb(scope, "kv", [P, NG, P + HG])
            x1_t = sb(scope, "x1_t", [P, NC, T])
            pre, low, exped, pos = ([sb(scope, f"{n}{i}", [P, HALF]) for i in range(2)]
                                    for n in ("pre", "low", "exped", "pos"))
            att = [sb(scope, f"att{i}", [P, D]) for i in range(2)]
            att_t = [sb(scope, f"att_t{i}", [P, NG, P]) for i in range(2)]
            den = sb(scope, "den", [P, H])
            rden = sb(scope, "rden", [P, H])
            q_hi = [sb(scope, f"q_hi{i}", [P, HALF], F32R) for i in range(2)]
            q_lo = [sb(scope, f"q_lo{i}", [P, HALF], F32R) for i in range(2)]
            x_in, xt_in, bias_in = stream("x_in"), streams_of("xt_in", B), stream("bias_in")

            def load_weight(name, src):
                return sp.dma(w_in[name], weights[name][:, :, :], t[src].rearrange("(c p) n -> p c n", p=P))

            ready = {}
            xt_ready = [None] * B
            ready["k"] = load_weight("k", "wk_t")
            xt_ready[0] = sp.dma(xt_in[0], x_t[0][:, :, :], t["x_t"][0].rearrange("(c p) n -> p c n", p=P))
            ready["v"] = load_weight("v", "wv_t")
            for n in ("k", "v", "o"):
                sp.dma(bias_in, bias_rows[n][:, :], t[f"L0_attn_b{n}"].partition_broadcast(P))
            sp.dma(bias_in, bq_col[:, :], t["bq_cols"])
            ready["q"] = load_weight("q", "wq_t")
            ready["o"] = load_weight("o", "wo_t")
            xt_ready[1] = sp.dma(xt_in[1], x_t[1][:, :, :], t["x_t"][1].rearrange("(c p) n -> p c n", p=P))
            ready["xq"] = load_weight("xq", "xwq_t")
            dve.wait(bias_in.all(), const_in.all())
            act.wait(bias_in.all())
            pool.wait(bias_in.all())
            ones_set = dve.run(V.memset, v_nat[:, :, :, P:P + 1], 1.0)
            pe.wait(ones_set)

            turn = 0

            def next_bank():
                nonlocal turn
                i = turn % 8
                turn += 1
                pe.wait(bank_free[i])
                return i

            exp_free = [None, None]
            for b in range(B):
                sp.wait(x1_out.all(), *([dve.last()] if b else []))
                xn_ready = sp.dma(x_in, x_nat[:, :, :], t["x"][b].rearrange("(n p) d -> p n d", p=P))
                pool.wait(xn_ready)
                for n in range(NT):
                    xb_ready = pool.run(G.tensor_tensor, x_nat[:, n, :], x_nat[:, n, :], bias_rows["o"][:, :],
                                        ALU.add)

                for n in range(NT):
                    pe.wait(ready["k"], xt_ready[b])
                    i = next_bank()
                    done = accumulate(bank(i), [(x_t[b][:, c, n * P:(n + 1) * P], weights["k"][:, c, :])
                                                for c in range(NC)])
                    s = n % 2
                    dve.wait(done)
                    a = dve.run(V.tensor_tensor, pre[s][:, :], bank(i), bias_rows["k"][:, :], ALU.add)
                    bank_free[i] = a
                    c_ = dve.then(V.tensor_scalar, low[s][:, :], pre[s][:, :], 0.0, None, ALU.min)
                    act.wait(c_, exp_free[s])
                    ex = act.run(S.activation, exped[s][:, :], low[s][:, :], ACT.Exp)
                    pe.wait(ready["v"])
                    i = next_bank()
                    done = accumulate(bank(i), [(x_t[b][:, c, n * P:(n + 1) * P], weights["v"][:, c, :])
                                                for c in range(NC)])
                    dve.wait(done)
                    bank_free[i] = dve.run(V.tensor_tensor, v_nat[:, n, :, 0:P],
                                           bank(i).rearrange("p (g e) -> p g e", g=NG),
                                           bias_rows["v"][:, :].rearrange("p (g e) -> p g e", g=NG), ALU.add)
                    dve.wait(ex)
                    kv_in = dve.run(V.scalar_tensor_tensor, k_nat[:, n, :], pre[s][:, :], 0.0, exped[s][:, :],
                                    ALU.max, ALU.add)
                    exp_free[s] = kv_in

                for g in range(NG):
                    pe.wait(kv_in)
                    i = next_bank()
                    done = accumulate(bank(i)[:, 0:P + 1], [(k_nat[:, n, g * P:(g + 1) * P], v_nat[:, n, g, :])
                                                            for n in range(NT)])
                    dve.wait(done)
                    dve.run(V.tensor_tensor, kv[:, g, 0:P], bank(i)[:, 0:P], same_head[:, :], ALU.mult)
                    kv_ready = bank_free[i] = dve.run(V.tensor_scalar, kv[:, g, P:P + HG], head_of[:, :],
                                                      bank(i)[:, P:P + 1], None, ALU.mult)

                for h in range(NH):
                    for g in range(NG):
                        s = g % 2
                        pe.wait(ready["q"])
                        i = next_bank()
                        done = accumulate(bank(i), [(weights["q"][:, c, g * P:(g + 1) * P],
                                                     x_t[b][:, c, h * HALF:(h + 1) * HALF]) for c in range(NC)])
                        dve.wait(done, exp_free[s])
                        lo_ = dve.run(V.tensor_scalar, low[s][:, :], bank(i), bq_col[:, g:g + 1], 0.0,
                                      ALU.add, ALU.min)
                        act.wait(lo_, exp_free[s])
                        act.run(S.activation, exped[s][:, :], low[s][:, :], ACT.Exp)
                        po = bank_free[i] = act.run(S.activation, pos[s][:, :], bank(i), ACT.Relu,
                                                    bias=bq_col[:, g:g + 1])
                        dve.wait(po)
                        q_ready = exp_free[s] = dve.run(V.tensor_tensor, q_t[:, g, h * HALF:(h + 1) * HALF],
                                                        pos[s][:, :], exped[s][:, :], ALU.add)

                pe.wait(kv_ready, q_ready)
                att_free = [None, None]
                for n in range(NT):
                    s = n % 2
                    dve.wait(att_free[s])
                    for pair in range(NG // 2):
                        i = next_bank()
                        for k in range(2):
                            g = 2 * pair + k
                            done = accumulate(bank(i)[:, k * (P + HG):(k + 1) * (P + HG)],
                                              [(q_t[:, g, n * P:(n + 1) * P], kv[:, g, :])])
                        both = bank(i)[:, 0:2 * (P + HG)].rearrange("p (k w) -> p k w", k=2)
                        hs = slice(pair * 2 * HG, (pair + 1) * 2 * HG)
                        dve.wait(done)
                        dve.run(V.tensor_scalar, den[:, hs].rearrange("p (k h) -> p k h", k=2),
                                both[:, :, P:P + HG], 1e-6, None, ALU.max)
                        dve.then(V.reciprocal, rden[:, hs], den[:, hs])
                        for k in range(2):
                            g = 2 * pair + k
                            bank_free[i] = att_done = dve.then(
                                V.tensor_tensor,
                                att[s][:, g * P:(g + 1) * P].rearrange("p (h e) -> p h e", h=HG),
                                both[:, k, 0:P].rearrange("p (h e) -> p h e", h=HG),
                                rden[:, g * HG:(g + 1) * HG].unsqueeze(2).to_broadcast([P, HG, DH]), ALU.mult)
                    pe.wait(att_done)
                    i = next_bank()
                    for g in range(NG):
                        issue = pe.run if g == NG - 1 else pe.quiet
                        done = issue(nc.tensor.transpose, bank(i)[:, g * P:(g + 1) * P],
                                     att[s][:, g * P:(g + 1) * P], identity[:, :])
                    att_free[s] = done
                    act.wait(done)
                    att_t_ready = bank_free[i] = act.run(S.activation, att_t[s][:, :, :].rearrange("p g n -> p (g n)"),
                                                         bank(i), ACT.Copy)
                    pe.wait(att_t_ready, ready["o"])
                    i = next_bank()
                    done = accumulate(bank(i), [(att_t[s][:, g, :], weights["o"][:, g, :]) for g in range(NG)])
                    dve.wait(done, xb_ready)
                    bank_free[i] = dve.run(V.tensor_tensor, x_nat[:, n, :], bank(i), x_nat[:, n, :], ALU.add)
                    tile_statistics(x_nat[:, n, :], n)
                    if n % (NT // 2) == NT // 2 - 1:
                        rs_done = rsqrt_of_variances(NT)if n == NT - 1 else rsqrt_of_variances(n + 1)
                        dve.wait(rs_done)
                        for m in range(n + 1 - NT // 2, n + 1):
                            x1_ready = normalise(x_nat[:, m, :], x_nat[:, m, :], m)
                            pe.wait(x1_ready)
                            i = next_bank()
                            for c in range(NC):
                                issue = pe.run if c == NC - 1 else pe.quiet
                                done = issue(nc.tensor.transpose, bank(i)[:, c * P:(c + 1) * P],
                                             x_nat[:, m, c * P:(c + 1) * P], identity[:, :])
                            act.wait(done)
                            x1_t_ready = bank_free[i] = act.run(
                                S.activation, x1_t[:, :, m * P:(m + 1) * P],
                                bank(i).rearrange("p (c n) -> p c n", c=NC), ACT.Copy)
                        h = n // (NT // 2)
                        lo_tile = n + 1 - NT // 2
                        sp.wait(x1_ready)
                        sp.dma(x1_out, x1_rows[b * T + lo_tile * P:b * T + (n + 1) * P, :]
                               .rearrange("(n p) d -> p n d", p=P), x_nat[:, lo_tile:n + 1, :])
                        pe.wait(x1_t_ready, ready["xq"])
                        for g in range(NG):
                            s2 = g % 2
                            i = next_bank()
                            done = accumulate(bank(i), [(weights["xq"][:, c, g * P:(g + 1) * P],
                                                         x1_t[:, c, h * HALF:(h + 1) * HALF]) for c in range(NC)])
                            act.wait(done, q_out[s2].all())
                            hi = act.run(S.activation, q_hi[s2][:, :], bank(i), ACT.Copy)
                            dve.wait(hi, q_out[s2].all())
                            bank_free[i] = lo_ = dve.run(V.tensor_tensor, q_lo[s2][:, :], bank(i),
                                                         q_hi[s2][:, :].bitcast(F32), ALU.subtract)
                            sp.wait(lo_)
                            for part, tile in enumerate((q_hi, q_lo)):
                                sp.dma(q_out[s2], q_parts[b, g * HG:(g + 1) * HG, part, :, h * HALF:(h + 1) * HALF],
                                       tile[s2][:, :].bitcast(F32))
            join()

        with ExitStack() as scope:
            xwk = sb(scope, "xwk_t", [P, NC, D])
            xwv = sb(scope, "xwv_t", [P, NC, D])
            ctx_t = [sb(scope, f"ctx_t{i}", [P, NC, HALF]) for i in range(2)]
            k_hi = [sb(scope, f"k_hi{i}", [P, HALF], F32R) for i in range(2)]
            k_lo = [sb(scope, f"k_lo{i}", [P, HALF], F32R) for i in range(2)]
            v_tile = [sb(scope, f"v_tile{i}", [P, D]) for i in range(2)]
            xw_in, ctx_in = stream("xw_in"), streams_of("ctx_in", 2)
            sp.dma(xw_in, xwk[:, :, :], t["xwk_t"].rearrange("(c p) n -> p c n", p=P))
            xw_ready = sp.dma(xw_in, xwv[:, :, :], t["xwv_t"].rearrange("(c p) n -> p c n", p=P))
            pe.wait(xw_ready)
            chunks = [(b, mc) for b in range(B) for mc in range(M // HALF)]
            ctx_free = [None, None]
            ctx_ready = {}

            def load_ctx(n):
                if n < len(chunks):
                    b, mc = chunks[n]
                    sp.wait(ctx_free[n % 2])
                    ctx_ready[n] = sp.dma(ctx_in[n % 2], ctx_t[n % 2][:, :, :],
                                          t["ctx_t"][b][:, mc * HALF:(mc + 1) * HALF]
                                          .rearrange("(c p) m -> p c m", p=P))

            load_ctx(0)
            load_ctx(1)
            for n, (b, mc) in enumerate(chunks):
                cs = ctx_t[n % 2]
                pe.wait(ctx_ready[n])
                for g in range(NG):
                    s = g % 2
                    i = next_bank()
                    done = accumulate(bank(i), [(xwk[:, c, g * P:(g + 1) * P], cs[:, c, :]) for c in range(NC)])
                    act.wait(done, k_out[s].all())
                    hi = act.run(S.activation, k_hi[s][:, :], bank(i), ACT.Copy)
                    dve.wait(hi, k_out[s].all())
                    bank_free[i] = lo_ = dve.run(V.tensor_tensor, k_lo[s][:, :], bank(i),
                                                 k_hi[s][:, :].bitcast(F32), ALU.subtract)
                    sp.wait(lo_)
                    for part, tile in enumerate((k_hi, k_lo)):
                        sp.dma(k_out[s], k_parts[b, g * HG:(g + 1) * HG, part, :, mc * HALF:(mc + 1) * HALF],
                               tile[s][:, :].bitcast(F32))
                for q in range(HALF // P):
                    s = q % 2
                    i = next_bank()
                    done = accumulate(bank(i), [(cs[:, c, q * P:(q + 1) * P], xwv[:, c, :]) for c in range(NC)])
                    act.wait(done, v_out[s].all())
                    vt = bank_free[i] = act.run(S.activation, v_tile[s][:, :], bank(i), ACT.Copy)
                    sp.wait(vt)
                    sp.dma(v_out[s], v_rows[b, :, :, mc * (HALF // P) + q, :].rearrange("g p e -> p g e"),
                           v_tile[s][:, :].rearrange("p (g e) -> p g e", g=NG))
                ctx_free[n % 2] = done
                load_ctx(n + 2)
            join()

        x2_out, table_out = stream("x2_out"), stream("table_out")
        with ExitStack() as scope:
            k_stack = [sb(scope, f"k_stack{i}", [P, HG, M], F32R) for i in range(2)]
            q_stack = [sb(scope, f"q_stack{i}", [P, HG, T], F32R) for i in range(2)]
            v_grp = [sb(scope, f"v_grp{i}", [P, MT, P]) for i in range(2)]
            NP = 4
            probs = [sb(scope, f"probs{i}", [P, HG, HALF]) for i in range(NP)]
            heads_t = sb(scope, "heads_t", [P, NG, T])
            xwo = sb(scope, "xwo_t", [P, NC, D])
            xbo_row = sb(scope, "xbo_row", [P, D])
            y_nat = sb(scope, "y_nat", [P, NT, D])
            num_c = sb(scope, "num_c", [P, HALF])
            den_c = sb(scope, "den_c", [P, HALF])
            max4 = sb(scope, "max4", [P, NT, HG, M // HALF])
            neg_max = sb(scope, "neg_max", [P, NT, HG])
            max_hi = sb(scope, "max_hi", [P, NT, HG], F32R)
            max_parts = sb(scope, "max_parts", [P, NT, SHIFT, HG])
            shift_rows = sb(scope, "shift_rows", [SHIFT * HG, T], F32R)
            x2_t = [sb(scope, f"x2_t{i}", [P, NC, P]) for i in range(2)]
            lg, ex8, pr, oh0, oh1, ms, sv, kp, tmp = (sb(scope, f"rt_{n}", [P, NT, E]) for n in
                                                     ("lg", "ex", "pr", "oh0", "oh1", "ms", "sv", "kp", "tmp"))
            top8 = sb(scope, "top8", [P, NT, 8])
            idx8 = sb(scope, "idx8", [P, NT, 8], U32)
            idxf = sb(scope, "idxf", [P, NT, 8])
            col = {n: sb(scope, f"col_{n}", [P, NT]) for n in ("max", "sum", "r", "s", "w", "k", "slot")}
            before = [sb(scope, f"before{i}", [P, E]) for i in range(2)]
            slot_i = sb(scope, "slot_i", [P, B * NT, TOPK], U32)
            entry = sb(scope, "entry", [P, B * NT, TOPK, 2], I32)

            groups = [(b, g) for b in range(B) for g in range(NG)]
            KCH = M // HALF
            k_in = [streams_of(f"k_in{i}_", KCH) for i in range(2)]
            q_in = [streams_of(f"q_in{i}_", NH) for i in range(2)]
            shift_in = streams_of("shift_in", 2)
            v_in = streams_of("v_in", 2)
            xwo_in, y_in = stream("xwo_in"), stream("y_in")
            k_ready, q_ready, v_ready, shift_ready = {}, {}, {}, {}

            one_rows = [dve.run(V.memset, k_stack[i][STK:STK + SHIFT, :, :].bitcast(F32), 1.0) for i in range(2)]
            zero_before = dve.run(V.memset, before[0][:, :], 0.0)
            pe.wait(*one_rows)

            def load_k(n, c, free=None):
                if n >= len(groups):
                    return
                b, g = groups[n]
                src = k_parts[b, g * HG:(g + 1) * HG, :, :, c * HALF:(c + 1) * HALF]
                dst = k_stack[n % 2][:, :, c * HALF:(c + 1) * HALF].bitcast(F32)
                sp.wait(free)
                sp.dma(k_in[n % 2][c], dst[0:2 * DH], src.rearrange("j l r m -> (l r) j m"))
                k_ready[n, c] = sp.dma(k_in[n % 2][c], dst[2 * DH:STK], src[:, 0].rearrange("j r m -> r j m"))

            def load_q(n, h, free=None):
                if n >= len(groups):
                    return
                b, g = groups[n]
                src = q_parts[b, g * HG:(g + 1) * HG, :, :, h * HALF:(h + 1) * HALF]
                dst = q_stack[n % 2][:, :, h * HALF:(h + 1) * HALF].bitcast(F32)
                sp.wait(free)
                sp.dma(q_in[n % 2][h], dst[0:DH], src[:, 0].rearrange("j r m -> r j m"))
                q_ready[n, h] = sp.dma(q_in[n % 2][h], dst[DH:STK], src.rearrange("j l r m -> (l r) j m"))

            def load_v(n, free=None):
                if n >= len(groups):
                    return
                b, g = groups[n]
                sp.wait(free)
                v_ready[n] = sp.dma(v_in[n % 2], v_grp[n % 2][:, :, :], v_rows[b, g])

            NUM, DEN = 6, 7

            class Ring:
                def __init__(self, *banks):
                    self.banks, self.turn = banks, 0

                def __call__(self):
                    i = self.banks[self.turn % len(self.banks)]
                    self.turn += 1
                    pe.wait(bank_free[i])
                    return i

            next_score_bank, next_s_bank = Ring(0, 1, 2), Ring(3, 4, 5)

            def max_pass(n):
                ks, qs = k_stack[n % 2], q_stack[n % 2]
                for mc in range(KCH):
                    pe.wait(k_ready[n, mc])
                    for nt in range(NT):
                        pe.wait(q_ready[n, nt * P // HALF])
                        for j in range(HG):
                            i = next_s_bank()
                            done = accumulate(bank(i), [(qs[0:STK, j, nt * P:(nt + 1) * P],
                                                         ks[0:STK, j, mc * HALF:(mc + 1) * HALF])])
                            dve.wait(done)
                            bank_free[i] = dve.run(V.reduce_max, max4[:, nt, j, mc:mc + 1], bank(i), AX.X)
                            yield

            shift_taken = [None]

            def shift_pass(n):
                dve.wait(shift_taken[0])
                dve.then(V.tensor_reduce, neg_max[:, :, :], max4[:, :, :, :], AX.X, ALU.max)
                dve.then(V.tensor_scalar, neg_max[:, :, :], neg_max[:, :, :], -1.0, None, ALU.mult)
                dve.then(V.tensor_copy, max_hi[:, :, :], neg_max[:, :, :])
                dve.then(V.tensor_copy, max_parts[:, :, 0, :], max_hi[:, :, :].bitcast(F32))
                parts_ready = dve.then(V.tensor_tensor, max_parts[:, :, 1, :], neg_max[:, :, :],
                                       max_hi[:, :, :].bitcast(F32), ALU.subtract)
                pe.wait(parts_ready)
                for h in range(NH):
                    i = next_s_bank()
                    for q in range(HALF // P):
                        nt = h * (HALF // P) + q
                        done = accumulate(bank(i)[0:SHIFT * HG, q * P:(q + 1) * P],
                                          [(max_parts[:, nt, :, :].rearrange("p l j -> p (l j)"), identity[:, :])])
                    act.wait(done, shift_in[(n - 1) % 2].all())
                    rows = bank_free[i] = act.run(S.activation, shift_rows[:, h * HALF:(h + 1) * HALF],
                                                  bank(i)[0:SHIFT * HG, :], ACT.Copy)
                shift_taken[0] = done
                sp.wait(rows, q_free[n % 2])
                for part in range(SHIFT):
                    shift_ready[n] = sp.dma(shift_in[n % 2], q_stack[n % 2][STK + part:STK + part + 1, :, :].bitcast(F32),
                                            shift_rows[part * HG:(part + 1) * HG, :].bitcast(F32))

            q_free = [None, None]
            probs_free = [None] * NP
            probs_turn = 0
            heads_free = None
            xwo_ready = sp.dma(xwo_in, xwo[:, :, :], t["xwo_t"].rearrange("(c p) n -> p c n", p=P))
            xwo_ready = sp.dma(xwo_in, xbo_row[:, :], t["L0_xattn_bo"].partition_broadcast(P))
            for n in range(2):
                for h in range(NH):
                    load_q(n, h)
                for c in range(KCH):
                    load_k(n, c)
                load_v(n)
            for _ in max_pass(0):
                pass
            shift_pass(0)

            def project_rows(b):
                sp.wait(x2_out.all(), dve.last())
                y_ready = sp.dma(y_in, y_nat[:, :, :], x1_rows[b * T:(b + 1) * T, :]
                                 .rearrange("(n p) d -> p n d", p=P))
                pool.wait(y_ready, xwo_ready)
                for n in range(NT):
                    yb = pool.run(G.tensor_tensor, y_nat[:, n, :], y_nat[:, n, :], xbo_row[:, :], ALU.add)
                pe.wait(heads_ready, xwo_ready)
                for n in range(NT):
                    i = next_s_bank()
                    done = accumulate(bank(i), [(heads_t[:, g, n * P:(n + 1) * P], xwo[:, g, :])
                                                for g in range(NG)])
                    dve.wait(done, yb)
                    bank_free[i] = dve.run(V.tensor_tensor, y_nat[:, n, :], bank(i), y_nat[:, n, :], ALU.add)
                    tile_statistics(y_nat[:, n, :], n)
                heads_done = done
                dve.wait(rsqrt_of_variances(NT))
                logit_bank = DEN
                pe.wait(bank_free[DEN])
                x2t_free = [None, None]
                for n in range(NT):
                    x2_ready = normalise(y_nat[:, n, :], y_nat[:, n, :], n)
                    pe.wait(x2_ready)
                    i = next_s_bank()
                    for c in range(NC):
                        issue = pe.run if c == NC - 1 else pe.quiet
                        done = issue(nc.tensor.transpose, bank(i)[:, c * P:(c + 1) * P],
                                     y_nat[:, n, c * P:(c + 1) * P], identity[:, :])
                    act.wait(done, x2t_free[n % 2])
                    xt = bank_free[i] = act.run(S.activation, x2_t[n % 2][:, :, :].rearrange("p c n -> p (c n)"),
                                                bank(i), ACT.Copy)
                    pe.wait(xt)
                    x2t_free[n % 2] = logits_done = accumulate(
                        bank(logit_bank)[:, n * E:(n + 1) * E],
                        [(x2_t[n % 2][:, c, :], router_w[:, c, :]) for c in range(NC)])
                sp.wait(x2_ready)
                for rows in (x2_rows, y_rows):
                    sp.dma(x2_out, rows[b * T:(b + 1) * T, :].rearrange("(n p) d -> p n d", p=P), y_nat[:, :, :])

                def per_tile(x):
                    return x[:, :].unsqueeze(2).to_broadcast([P, NT, E])

                def per_expert(x):
                    return x[:, :].unsqueeze(1).to_broadcast([P, NT, E])

                def third(x, k):
                    return x[:, :, k:k + 1].to_broadcast([P, NT, E])

                dve.wait(logits_done)
                bank_free[DEN] = dve.then(V.tensor_tensor, lg[:, :, :],
                                          bank(DEN)[:, 0:NT * E].rearrange("p (n e) -> p n e", n=NT),
                                          per_expert(router_bias), ALU.add)
                dve.then(V.reduce_max, col["max"][:, :], lg[:, :, :], AX.X)
                lg_ready = dve.then(V.tensor_tensor, lg[:, :, :], lg[:, :, :], per_tile(col["max"]), ALU.subtract)
                act.wait(lg_ready)
                ex_ready = act.run(S.activation, ex8[:, :, :], lg[:, :, :], ACT.Exp)
                dve.wait(ex_ready)
                dve.then(V.reduce_sum, col["sum"][:, :], ex8[:, :, :], AX.X)
                dve.then(V.reciprocal, col["r"][:, :], col["sum"][:, :])
                pr_ready = dve.then(V.tensor_tensor, pr[:, :, :], ex8[:, :, :], per_tile(col["r"]), ALU.mult)
                dve.wait(pr_ready)
                for n in range(NT):
                    top_done = dve.run(V.max, top8[:, n, :], pr[:, n, :])
                dve.wait(top_done)
                for n in range(NT):
                    dve.run(V.max_index, idx8[:, n, :], top8[:, n, :], pr[:, n, :])
                dve.then(V.tensor_copy, idxf[:, :, :], idx8[:, :, :])
                dve.then(V.tensor_tensor, oh0[:, :, :], per_expert(expert_no), third(idxf, 0), ALU.is_equal)
                dve.then(V.tensor_tensor, oh1[:, :, :], per_expert(expert_no), third(idxf, 1), ALU.is_equal)
                ms_ready = dve.then(V.tensor_tensor, ms[:, :, :], oh0[:, :, :], oh1[:, :, :], ALU.add)
                pe.wait(ms_ready, bank_free[DEN])
                for n in range(NT):
                    k = (b * NT + n) % 2
                    pe.wait(dve.last())
                    ranks_done = accumulate(bank(DEN)[:, n * E:(n + 1) * E],
                                            [(earlier[:, :], ms[:, n, :]), (ones[:, :], before[k][:, :])])
                    dve.wait(ranks_done)
                    dve.then(V.tensor_tensor, before[1 - k][:, :], before[k][:, :], ms[:, n, :], ALU.add)
                rank = bank(DEN)[:, 0:NT * E].rearrange("p (n e) -> p n e", n=NT)
                dve.wait(ranks_done)
                dve.then(V.tensor_scalar, kp[:, :, :], rank, float(CAP), None, ALU.is_lt)
                bank_free[DEN] = dve.then(V.tensor_tensor, sv[:, :, :], rank, per_expert(expert_base), ALU.add)
                dve.then(V.tensor_tensor, col["s"][:, :], top8[:, :, 0], top8[:, :, 1], ALU.add)
                dve.then(V.tensor_scalar, col["s"][:, :], col["s"][:, :], 1e-9, None, ALU.max)
                dve.then(V.reciprocal, col["r"][:, :], col["s"][:, :])
                tiles = slice(b * NT, (b + 1) * NT)
                for k, oh in enumerate((oh0, oh1)):
                    dve.then(V.tensor_tensor, tmp[:, :, :], oh[:, :, :], sv[:, :, :], ALU.mult)
                    dve.then(V.reduce_sum, col["slot"][:, :], tmp[:, :, :], AX.X)
                    dve.then(V.tensor_tensor, tmp[:, :, :], oh[:, :, :], kp[:, :, :], ALU.mult)
                    dve.then(V.reduce_sum, col["k"][:, :], tmp[:, :, :], AX.X)
                    dve.then(V.tensor_scalar, col["slot"][:, :], col["slot"][:, :], dump_slot[:, :], None,
                             ALU.subtract)
                    dve.then(V.tensor_tensor, col["slot"][:, :], col["slot"][:, :], col["k"][:, :], ALU.mult)
                    dve.then(V.tensor_scalar, col["slot"][:, :], col["slot"][:, :], dump_slot[:, :], None, ALU.add)
                    dve.then(V.tensor_copy, slot_i[:, tiles, k], col["slot"][:, :])
                    dve.then(V.tensor_tensor, entry[:, tiles, k, 1].bitcast(F32), top8[:, :, k], col["r"][:, :],
                             ALU.mult)
                    entry_ready = dve.then(V.tensor_copy, entry[:, tiles, k, 0], token_id[:, tiles])
                pool.wait(entry_ready, scratch_init.all())
                for n in range(b * NT, (b + 1) * NT):
                    for k in range(TOPK):
                        pool.wait(table_out.all())
                        pool.indirect(table_out, out=slot_table,
                                      out_offset=bass.IndirectOffsetOnAxis(ap=slot_i[:, n, k:k + 1], axis=0),
                                      in_=entry[:, n, k, :], in_offset=None)
                return heads_done

            divisions = []
            PIECE = HALF // 8

            def divide(pieces):
                nonlocal heads_ready
                for _ in range(min(pieces, len(divisions))):
                    copied, g, h, q = divisions.pop(0)
                    dve.wait(copied, heads_free)
                    cols = slice(q * PIECE, (q + 1) * PIECE)
                    dve.run(V.reciprocal, den_c[:, cols], den_c[:, cols])
                    heads_ready = dve.then(V.tensor_tensor, heads_t[:, g, h * HALF + q * PIECE:h * HALF + (q + 1) * PIECE],
                                           num_c[:, cols], den_c[:, cols], ALU.mult)

            pending = []
            clock = 0

            def denominators(until):
                while pending and pending[0][0] <= until:
                    _, q, summed, mt, g, h = pending.pop(0)
                    pe.wait(summed)
                    if mt == 1:
                        pe.wait(bank_free[DEN])
                    for j in range(HG):
                        den_done = accumulate(bank(DEN)[j * DH:(j + 1) * DH, :],
                                              [(ones[:, 0:DH], probs[q][:, j, :])],
                                              start=mt == 1, stop=mt == MT - 1)
                    probs_free[q] = (den_done,)
                    if mt == MT - 1:
                        act.wait(den_done, heads_ready)
                        bank_free[DEN] = copied = act.run(S.activation, den_c[:, :], bank(DEN), ACT.Copy)
                        divisions.extend((copied, g, h, q) for q in range(HALF // PIECE))

            heads_ready = None
            for n, (b, g) in enumerate(groups):
                ks, qs, vs = k_stack[n % 2], q_stack[n % 2], v_grp[n % 2]
                ahead = max_pass(n + 1) if n + 1 < len(groups) else None
                todo = KCH * NT * HG if ahead else 0
                steps = [(h, mt) for h in range(NH) for mt in range(MT)]
                FIRST, LAST = 0, 28
                issued = 0
                allowed = 0

                def maxima(count=1):
                    nonlocal issued, ahead
                    while ahead and count and issued < allowed:
                        next(ahead)
                        issued += 1
                        count -= 1
                    if ahead and issued == todo:
                        for _ in ahead:
                            pass
                        shift_pass(n + 1)
                        ahead = None

                def scores(h, mt, p, heads):
                    pe.wait(k_ready[n, mt * P // HALF], q_ready[n, h], shift_ready[n])
                    act.wait(*(probs_free[p] or ()))
                    for j in heads:
                        i = next_score_bank()
                        done = accumulate(bank(i), [(ks[0:STK + SHIFT, j, mt * P:(mt + 1) * P],
                                                     qs[0:STK + SHIFT, j, h * HALF:(h + 1) * HALF])])
                        act.wait(done)
                        exp_done = bank_free[i] = act.run(S.activation, probs[p][:, j, :], bank(i), ACT.Exp,
                                                          scale=SCALE)
                    maxima()
                    return p, exp_done, done

                def next_probs():
                    nonlocal probs_turn
                    probs_turn += 1
                    return (probs_turn - 1) % NP

                current = scores(*steps[0], next_probs(), range(HG))
                for s, (h, mt) in enumerate(steps):
                    p, exp_done, _ = current
                    denominators(clock)
                    maxima()
                    if ahead:
                        allowed = min(todo, -(-todo * (s + 1 - FIRST) // (LAST - FIRST)))
                    if s + 1 < len(steps):
                        p_next = next_probs()
                        scores(*steps[s + 1], p_next, range(HG // 2))
                    pe.wait(exp_done, v_ready[n])
                    if mt == 0:
                        pe.wait(bank_free[NUM])
                    for j in range(HG):
                        num_done = accumulate(bank(NUM)[j * DH:(j + 1) * DH, :],
                                              [(vs[:, mt, j * DH:(j + 1) * DH], probs[p][:, j, :])],
                                              start=mt == 0, stop=mt == MT - 1)
                    maxima()
                    if s + 1 < len(steps):
                        following = scores(*steps[s + 1], p_next, range(HG // 2, HG))
                        h2, mt2 = steps[s + 1]
                        if h2 == NH - 1 and mt2 % (HALF // P) == HALF // P - 1:
                            load_k(n + 2, mt2 * P // HALF, following[2])
                    if s == MT - 1:
                        load_q(n + 2, 0, following[2])
                    if mt % 2 == 0:
                        even = p, num_done
                    else:
                        pool.wait(exp_done, even[1])
                        summed = pool.run(G.tensor_tensor, probs[even[0]][:, :, :], probs[even[0]][:, :, :],
                                          probs[p][:, :, :], ALU.add)
                        probs_free[p] = (num_done, summed)
                        pending.append((clock + 2, even[0], summed, mt, g, h))
                    maxima(2)
                    divide(1)
                    if mt == MT - 1:
                        divide(len(divisions))
                        act.wait(num_done, heads_ready)
                        bank_free[NUM] = act.run(S.activation, num_c[:, :], bank(NUM), ACT.Copy)
                    clock += 1
                    current = following
                q_free[n % 2] = current[2]
                load_q(n + 2, 1, current[2])
                load_v(n + 2, num_done)
                if g == NG - 1:
                    denominators(clock + 3)
                    divide(len(divisions))
                    heads_free = project_rows(b)
            join()

        y_add, out_done = stream("y_add"), streams_of("out_done", 2)
        with ExitStack() as scope:
            w1s = [sb(scope, f"w1s{i}", [P, NC, F]) for i in range(2)]
            w2s = [sb(scope, f"w2s{i}", [P, NF, D]) for i in range(2)]
            b2s = [sb(scope, f"b2s{i}", [P, D]) for i in range(2)]
            b1c = sb(scope, "b1c", [P, E, NF])
            table = sb(scope, "table", [P, E * NS, 2], I32)
            tok = sb(scope, "tok", [P, E * NS], U32)
            xg = [sb(scope, f"xg{i}", [P, D]) for i in range(2 * NS)]
            xe_t = [sb(scope, f"xe_t{i}", [P, NC, CAP]) for i in range(2)]
            hid_t = sb(scope, "hid_t", [P, NF, CAP])
            eo = [sb(scope, f"eo{i}", [P, D]) for i in range(3)]
            w_in = streams_of("we_in", 2)
            b1_in, table_in = stream("b1_in"), stream("table_in")
            xg_in = streams_of("xg_in", 2 * NS)
            w_ready, xg_ready = {}, {}
            w_free = [None, None]

            def load_expert(e):
                if e < E:
                    sp.wait(*(w_free[e % 2] or ()))
                    sp.dma(w_in[e % 2], w1s[e % 2][:, :, :], t["L0_ffn_w1"][e].rearrange("(c p) f -> p c f", p=P))
                    sp.dma(w_in[e % 2], w2s[e % 2][:, :, :], t["L0_ffn_w2"][e].rearrange("(c p) d -> p c d", p=P))
                    w_ready[e] = sp.dma(w_in[e % 2], b2s[e % 2][:, :], t["L0_ffn_b2"][e].partition_broadcast(P))

            table_ready = sp.dma(table_in, table[:, :, :].rearrange("p (e i) w -> p e i w", e=E),
                                 slot_table[0:SLOTS, :].rearrange("(e p i) w -> p e i w", p=P, i=NS))
            b1_ready = sp.dma(b1_in, b1c[:, :, :], t["b1_cols"])
            load_expert(0)
            load_expert(1)
            dve.wait(table_ready)
            tok_ready = dve.run(V.tensor_copy, tok[:, :], table[:, :, 0])
            pool.wait(tok_ready)
            act.wait(b1_ready)
            xg_free = [None] * (2 * NS)

            def gather(e):
                if e < E:
                    for i in range(NS):
                        s = (e % 2) * NS + i
                        pool.wait(xg_free[s])
                        xg_ready[e, i] = pool.indirect(
                            xg_in[s], out=xg[s][:, :], out_offset=None, in_=x2_rows,
                            in_offset=bass.IndirectOffsetOnAxis(ap=tok[:, e * NS + i:e * NS + i + 1], axis=0))

            TB, HB, OB = (4, 5), (0, 1), (6, 7)
            t_turn = 0
            xe_ready = {}

            def transposes(e):
                nonlocal t_turn
                if e >= E:
                    return
                for i in range(NS):
                    s = (e % 2) * NS + i
                    k = TB[t_turn % 2]
                    t_turn += 1
                    pe.wait(xg_ready[e, i], bank_free[k])
                    for c in range(NC):
                        issue = pe.run if c == NC - 1 else pe.quiet
                        done = issue(nc.tensor.transpose, bank(k)[:, c * P:(c + 1) * P],
                                     xg[s][:, c * P:(c + 1) * P], identity[:, :])
                    xg_free[s] = done
                    dve.wait(done)
                    xe_ready[e] = bank_free[k] = dve.run(V.tensor_copy, xe_t[e % 2][:, :, i * P:(i + 1) * P],
                                                         bank(k).rearrange("p (c n) -> p c n", c=NC))

            gather(0)
            gather(1)
            transposes(0)
            eo_turn = 0
            eo_free = [None] * 3
            HC = CAP // 2
            for e in range(E):
                xe, w1e, w2e = xe_t[e % 2], w1s[e % 2], w2s[e % 2]
                pe.wait(w_ready[e], xe_ready[e])
                for f in range(NF):
                    pr_ = HB[f % 2]
                    pe.wait(bank_free[2 * pr_])
                    for c in range(NC):
                        for h in range(2):
                            issue = pe.run if (c, h) == (NC - 1, 1) else pe.quiet
                            done = issue(nc.tensor.matmul, pairs[pr_][:, h, 0:HC], w1e[:, c, f * P:(f + 1) * P],
                                         xe[:, c, h * HC:(h + 1) * HC], start=c == 0, stop=c == NC - 1)
                    act.wait(done)
                    hid_ready = bank_free[2 * pr_] = bank_free[2 * pr_ + 1] = act.run(
                        S.activation, hid_t[:, f, :].rearrange("p (h n) -> p h n", h=2), pairs[pr_][:, :, 0:HC],
                        ACT.Gelu, bias=b1c[:, e, f:f + 1])
                gather(e + 2)
                transposes(e + 1)
                pe.wait(hid_ready)
                for i in range(NS):
                    k = OB[i % 2]
                    pe.wait(bank_free[k])
                    done = accumulate(bank(k), [(hid_t[:, f, i * P:(i + 1) * P], w2e[:, f, :]) for f in range(NF)])
                    s = eo_turn % 3
                    eo_turn += 1
                    dve.wait(done, w_ready[e], eo_free[s])
                    bank_free[k] = dve.run(V.tensor_tensor, eo[s][:, :], bank(k), b2s[e % 2][:, :], ALU.add)
                    eo_ready = dve.then(V.tensor_scalar, eo[s][:, :], eo[s][:, :],
                                        table[:, e * NS + i, 1:2].bitcast(F32), None, ALU.mult)
                    pool.wait(eo_ready, y_add.all())
                    eo_free[s] = pool.indirect(
                        y_add, out=y_rows, in_=eo[s][:, :], in_offset=None, compute_op=ALU.add,
                        out_offset=bass.IndirectOffsetOnAxis(ap=tok[:, e * NS + i:e * NS + i + 1], axis=0))
                w_free[e % 2] = (done, eo_ready)
                act.wait(done)
                load_expert(e + 2)
            added = y_add.all()
            join()

        with ExitStack() as scope:
            yf = sb(scope, "y_final", [P, B * NT, D])
            y_in2 = streams_of("yf_in", 4)
            Q4 = B * NT // 4
            for q in range(4):
                rows = y_rows[q * Q4 * P:(q + 1) * Q4 * P, :].rearrange("(n p) d -> p n d", p=P)
                sp.wait(added)
                sp.dma(y_in2[q], yf[:, q * Q4:(q + 1) * Q4, :], rows)
            out_flat = t["out"].rearrange("b s d -> (b s) d")
            for q in range(4):
                dve.wait(y_in2[q].all())
                for n in range(Q4):
                    dve.then(V.bn_stats, stats[:, :], yf[:, q * Q4 + n, :])
                    dve.then(V.bn_aggr, mean_var[:, n, :], stats[:, :])
                dve.wait(rsqrt_of_variances(Q4))
                for n in range(Q4):
                    done = normalise(yf[:, q * Q4 + n, :], yf[:, q * Q4 + n, :], n)
                act.wait(done)
                act.dma(out_done[q % 2], out_flat[q * Q4 * P:(q + 1) * Q4 * P, :].rearrange("(n p) d -> p n d", p=P),
                        yf[:, q * Q4:(q + 1) * Q4, :])
            act.wait(*[s.all() for s in streams])

        block = ctx.enter_context(nc.Block())

        @block.tensor
        def _(_eng):
            pe.emit()

        @block.vector
        def _(_eng):
            dve.emit()

        @block.scalar
        def _(_eng):
            act.emit()

        @block.gpsimd
        def _(_eng):
            pool.emit()

        @block.sync
        def _(_eng):
            sp.emit()


def kernel(**inputs):
    import concourse.bacc as _bacc
    from concourse.bass_utils import run_bass_kernel_spmd as _run

    arrays = {n: np.ascontiguousarray(inputs[n]) for n in (
        "x", "L0_attn_bk", "L0_attn_bv", "L0_attn_bo", "L0_xattn_bo", "L0_ffn_router_w",
        "L0_ffn_router_b", "L0_ffn_w1", "L0_ffn_w2", "L0_ffn_b2")}
    arrays["x_t"] = np.ascontiguousarray(np.transpose(inputs["x"], (0, 2, 1)))
    arrays["ctx_t"] = np.ascontiguousarray(np.transpose(inputs["ctx_1024"], (0, 2, 1)))
    arrays["bq_cols"] = np.ascontiguousarray(np.reshape(inputs["L0_attn_bq"], (NG, P)).transpose(1, 0))
    arrays["b1_cols"] = np.ascontiguousarray(np.reshape(inputs["L0_ffn_b1"], (E, NF, P)).transpose(2, 0, 1))
    for short, name in (("wq_t", "L0_attn_Wq"), ("wk_t", "L0_attn_Wk"), ("wv_t", "L0_attn_Wv"),
                        ("wo_t", "L0_attn_Wo"), ("xwq_t", "L0_xattn_wq"), ("xwk_t", "L0_xattn_wk"),
                        ("xwv_t", "L0_xattn_wv"), ("xwo_t", "L0_xattn_wo")):
        arrays[short] = np.ascontiguousarray(np.transpose(inputs[name], (1, 0)))
    lane, f32 = np.arange(P), np.float32
    arrays["identity"] = np.eye(P, dtype=f32)
    arrays["same_head"] = (lane[:, None] // DH == lane[None, :] // DH).astype(f32)
    arrays["head_of"] = (lane[:, None] // DH == np.arange(HG)[None, :]).astype(f32)
    arrays["earlier"] = (lane[:, None] < lane[None, :]).astype(f32)
    arrays["ones"] = np.ones((P, P), f32)
    arrays["zeros"] = np.zeros((P, D), f32)
    arrays["expert_no"] = np.tile(np.arange(E, dtype=f32), (P, 1))
    arrays["expert_base"] = np.tile(np.arange(E, dtype=f32) * CAP, (P, 1))
    arrays["token_id"] = (np.arange(B * NT)[None, :] * P + lane[:, None]).astype(np.int32)
    arrays["dump_slot"] = (SLOTS + lane[:, None]).astype(f32)
    init = np.zeros((SLOTS + P, 2), np.int32)
    init[:SLOTS, 0] = NTOK + np.tile(np.repeat(lane, NS), E)
    arrays["table_init"] = init

    nc = _bacc.Bacc("TRN2", target_bir_lowering=False, num_devices=1)
    t, ins = {}, {}
    for name, a in arrays.items():
        t[name] = nc.dram_tensor(f"in_{name}", a.shape, mybir.dt.from_np(a.dtype), kind="ExternalInput").ap()
        ins[f"in_{name}"] = a
    t["out"] = nc.dram_tensor("out_0", (B, T, D), F32, kind="ExternalOutput").ap()
    program(nc, t)
    r = _run(nc, [ins], core_ids=[0])
    return r.results[0]["out_0"]
```

```python
import numpy as np
from contextlib import ExitStack

import concourse.bass as bass
from concourse import mybir

F32 = mybir.dt.float32
F32R = mybir.dt.float32r
I32 = mybir.dt.int32
U32 = mybir.dt.uint32
ALU = mybir.AluOpType
ACT = mybir.ActivationFunctionType
AX = mybir.AxisListType

P = 128
B, T, M, D = 2, 1024, 2048, 512
H, DH = 16, 32
HG = P // DH
NG = H // HG
NC = D // P
NT = T // P
NTOK = B * T
MT = M // P
HALF = 512
NH = T // HALF
E, F, TOPK = 8, 1024, 2
NF = F // P
CAP = -(-5 * NTOK * TOPK // (4 * E))
NS = CAP // P
SLOTS = E * CAP
TABLES = 4
SCALE = float(DH) ** -0.5
EPS = 1e-5
STK = 3 * DH
SHIFT = 2
RSQRT_MAGIC = 0x5F3759DF


class Engine:

    def __init__(self, handle, sem):
        self.handle, self.sem, self.count, self.queue, self.seen = handle, sem, 0, [], {}

    def wait(self, *tokens):
        for token in tokens:
            if token is None:
                continue
            sem, value = token
            if self.seen.get(id(sem), 0) < value:
                self.seen[id(sem)] = value
                self.queue.append((None, (sem, value), {}, None, 0))

    def quiet(self, fn, *args, **kw):
        self.queue.append((fn, args, kw, None, 0))

    def run(self, fn, *args, **kw):
        self.count += 1
        self.queue.append((fn, args, kw, self.sem, 1))
        return (self.sem, self.count)

    def then(self, fn, *args, **kw):
        if self.count:
            self.wait((self.sem, self.count))
        return self.run(fn, *args, **kw)

    def dma(self, stream, out, in_, **kw):
        stream.count += 16
        self.queue.append((self.handle.dma_start, (out, in_), kw, stream.sem, 16))
        return (stream.sem, stream.count)

    def indirect(self, stream, **kw):
        stream.count += 16
        self.queue.append((self.handle.indirect_dma_start, (), kw, stream.sem, 16))
        return (stream.sem, stream.count)

    def last(self):
        return (self.sem, self.count) if self.count else None

    def emit(self):
        for fn, args, kw, sem, by in self.queue:
            if fn is None:
                self.handle.wait_ge(*args)
            elif sem is None:
                fn(*args, **kw)
            else:
                fn(*args, **kw).then_inc(sem, by)


class Stream:

    def __init__(self, sem):
        self.sem, self.count = sem, 0

    def all(self):
        return (self.sem, self.count) if self.count else None


def program(nc, t):
    ctx = ExitStack()
    with ctx:
        def sem(name):
            return ctx.enter_context(nc.semaphore(name))

        pe = Engine(nc.tensor, sem("pe_done"))
        dve = Engine(nc.vector, sem("dve_done"))
        act = Engine(nc.scalar, sem("act_done"))
        pool = Engine(nc.gpsimd, sem("pool_done"))
        sp = Engine(nc.sync, sem("sp_done"))
        engines = [pe, dve, act, pool, sp]
        streams = []

        def stream(name):
            streams.append(Stream(sem(name)))
            return streams[-1]

        def streams_of(name, n):
            return [stream(f"{name}{i}") for i in range(n)]

        def sb(scope, name, shape, dt=F32):
            return scope.enter_context(nc.sbuf_tensor(name, shape, dt))

        V, S, G = nc.vector, nc.scalar, nc.gpsimd

        q_parts = nc.dram_tensor("q_parts", (B, H, 2, DH, T), F32).ap()
        k_parts = nc.dram_tensor("k_parts", (B, H, 2, DH, M), F32).ap()
        v_rows = nc.dram_tensor("v_rows", (B, NG, P, MT, P), F32).ap()
        x1_rows = nc.dram_tensor("x1_rows", (NTOK, D), F32).ap()
        x2_rows = nc.dram_tensor("x2_rows", (NTOK + P, D), F32).ap()
        y_rows = nc.dram_tensor("y_rows", (NTOK + P, D), F32).ap()
        slot_tables = [nc.dram_tensor(f"slot_table{i}", (SLOTS + P, 2), F32).ap() for i in range(TABLES)]

        pairs = [ctx.enter_context(nc.psum_tensor(f"banks{2 * i}", [P, 2, HALF], F32)) for i in range(4)]
        bank_free = [None] * 8

        def bank(i):
            return pairs[i // 2][:, i % 2, :]

        def accumulate(out, operands, start=True, stop=True):
            for n, (lhsT, rhs) in enumerate(operands):
                first, last = start and n == 0, stop and n == len(operands) - 1
                issue = pe.run if n == len(operands) - 1 else pe.quiet
                done = issue(nc.tensor.matmul, out, lhsT, rhs, start=first, stop=last)
            return done

        identity = sb(ctx, "identity", [P, P])
        same_head = sb(ctx, "same_head", [P, P])
        head_of = sb(ctx, "head_of", [P, HG])
        earlier = sb(ctx, "earlier", [P, P])
        ones = sb(ctx, "ones", [P, P])
        expert_no = sb(ctx, "expert_no", [P, E])
        expert_base = sb(ctx, "expert_base", [P, E])
        router_bias = sb(ctx, "router_bias", [P, E])
        router_w = sb(ctx, "router_w", [P, NC, E])
        token_no = sb(ctx, "token_no", [P, B * NT])
        empty_row = sb(ctx, "empty_row", [P, 1])
        dump_slot = sb(ctx, "dump_slot", [P, 1])
        stats = sb(ctx, "stats", [P, 6])
        mean_var = sb(ctx, "mean_var", [P, NT, 2])
        rs_a, rs_b, rs_y = (sb(ctx, f"rsqrt_{n}", [P, NT]) for n in ("a", "b", "y"))
        const_in = stream("const_in")
        for tile, src in ((identity, t["identity"]), (same_head, t["same_head"]), (head_of, t["head_of"]),
                          (earlier, t["earlier"]), (ones, t["ones"]), (expert_no, t["expert_no"]),
                          (expert_base, t["expert_base"]), (token_no, t["token_no"]),
                          (dump_slot, t["dump_slot"]), (empty_row, t["empty_row"])):
            pool.dma(const_in, tile[:, :], src)
        pool.dma(const_in, router_bias[:, :], t["L0_ffn_router_b"].partition_broadcast(P))
        pool.dma(const_in, router_w[:, :, :], t["L0_ffn_router_w"].rearrange("(c p) e -> p c e", p=P))
        scratch_init = stream("scratch_init")
        for table in slot_tables:
            pool.dma(scratch_init, table, t["table_init"])
        pool.dma(scratch_init, x2_rows[NTOK:, :], t["zeros"])
        pool.dma(scratch_init, y_rows[NTOK:, :], t["zeros"])

        class Shelf:

            def __init__(self, at):
                self.at = at

            def __call__(self, name, shape, dt=F32):
                tensor = nc.alloc_sbuf_tensor_at(name, shape, dt, offset=self.at)
                size = 4 * int(np.prod(shape[1:]))
                self.at += -(-size // 32) * 32
                assert self.at <= nc.sbuf_top, name
                return tensor

        def rsqrt_of_variances(n):
            var, a, b, y = mean_var[:, 0:n, 1], rs_a[:, 0:n], rs_b[:, 0:n], rs_y[:, 0:n]
            dve.then(V.tensor_scalar, a, var, EPS, None, ALU.add)
            dve.then(V.tensor_scalar, y.bitcast(I32), a.bitcast(I32), 1, None, ALU.logical_shift_right)
            dve.then(V.tensor_scalar, y.bitcast(I32), y.bitcast(I32), -1.0, float(RSQRT_MAGIC), ALU.mult, ALU.add)
            dve.then(V.tensor_scalar, a, a, -0.5, None, ALU.mult)
            for _ in range(4):
                dve.then(V.tensor_tensor, b, y, y, ALU.mult)
                dve.then(V.tensor_tensor, b, b, a, ALU.mult)
                done = dve.then(V.scalar_tensor_tensor, y, b, 1.5, y, ALU.add, ALU.mult)
            return done

        def tile_statistics(row, n):
            dve.then(V.bn_stats, stats[:, :], row)
            return dve.then(V.bn_aggr, mean_var[:, n, :], stats[:, :])

        def normalise(out, row, n):
            return dve.run(V.tensor_scalar, out, row, mean_var[:, n, 0:1], rs_y[:, n:n + 1],
                           ALU.subtract, ALU.mult)

        def join(*extra):
            ends = [x.last() for x in engines] + [s.all() for s in streams] + list(extra)
            for engine in engines:
                engine.wait(*ends)

        HT = NT // NH
        b1c = sb(ctx, "b1c", [P, E, NF])
        table = sb(ctx, "table", [P, TABLES, E * NS, 2])
        tok = sb(ctx, "tok", [P, E * NS], U32)
        max4 = sb(ctx, "max4", [P, NT, HG, M // HALF])
        neg_max = sb(ctx, "neg_max", [P, NT, HG])
        max_hi = sb(ctx, "max_hi", [P, NT, HG], F32R)
        max_parts = sb(ctx, "max_parts", [P, NT, SHIFT, HG])
        TAIL_BYTES = 53504
        tail_base = (nc.sbuf_top - TAIL_BYTES) // 32 * 32
        loop_base = -(-nc.sbuf_base // 32) * 32

        put = Shelf(loop_base)
        NP = 4
        k_stack, q_stack = [put("k_stack0", [P, HG, M], F32R)], [put("q_stack0", [P, HG, T], F32R)]
        v_grp = [put(f"v_grp{i}", [P, MT, P]) for i in range(2)]
        probs = [put(f"probs{i}", [P, HG, HALF]) for i in range(NP)]
        shift_rows = put("shift_rows", [SHIFT * HG, T], F32R)
        context_base = put.at
        q_stack.append(put("q_stack1", [P, HG, T], F32R))
        k_stack.append(put("k_stack1", [P, HG, M], F32R))
        assert put.at <= tail_base
        put = Shelf(tail_base)
        heads_t = put("heads_t", [P, NG, T])
        xwo = put("xwo_t", [P, NC, D])
        xbo_row = put("xbo_row", [P, D])
        y_nat = [put(f"y_nat{i}", [P, HT, D]) for i in range(NH)]
        x2_t = [put(f"x2_t{i}", [P, NC, P]) for i in range(2)]
        num_c = put("num_c", [P, HALF])
        den_c = put("den_c", [P, HALF])
        lg, ex8, pr, oh0, oh1, ms, sv, kp, picked = (put(f"rt_{n}", [P, HT, E]) for n in
                                                     ("lg", "ex", "pr", "oh0", "oh1", "ms", "sv", "kp", "picked"))
        top8 = put("top8", [P, HT, 8])
        idx8 = put("idx8", [P, HT, 8], U32)
        idxf = put("idxf", [P, HT, 8])
        col = {n: put(f"col_{n}", [P, HT]) for n in ("max", "sum", "r", "s", "w", "k", "slot")}
        before = put("before", [P, HT + 1, E])
        slot_i = put("slot_i", [P, B * NT, TOPK], U32)
        entry = put("entry", [P, B * NT, TOPK, 2])

        put = Shelf(context_base)
        w_parts = {"k": [put(f"wk_{p}", [P, NC, D], F32R) for p in ("hi", "lo")],
                   "v": [put(f"wv_{p}", [P, NC, D], F32R) for p in ("hi", "lo")]}
        raw = [put(f"raw{i}", [P, NC, HALF]) for i in range(2)]
        src_parts = [[put(f"src{i}_{p}", [P, NC, HALF], F32R) for p in ("hi", "lo")] for i in range(2)]
        out_parts = [[put(f"out{i}_{p}", [P, HALF], F32R) for p in ("hi", "lo")] for i in range(2)]
        pre = [put(f"pre{i}", [P, HALF]) for i in range(2)]
        kv = put("kv", [P, NG, P + HG])
        kv_part = put("kv_part", [P, NG, P + 1])
        att_t = put("att_t", [P, NG, P])
        att = [put(f"att{i}", [P, D]) for i in range(2)]
        put = Shelf(loop_base)
        w_parts["q"] = [put(f"wq_{p}", [P, NC, D], F32R) for p in ("hi", "lo")]
        wo, wxq = put("wo", [P, NC, D]), put("wxq", [P, NC, D])
        k_half = put("k_half", [P, HT, D])
        v_half_at = put.at
        v_half = put("v_half", [P, HT, NG, P + 1])
        q_t_at = put.at
        q_t = put("q_t", [P, NG, T])
        x_nat = [put(f"x_nat{h}", [P, HT, D]) for h in range(NH)]
        x1_t = put("x1_t", [P, NC, HALF])
        low = [put(f"low{i}", [P, HALF]) for i in range(2)]
        bias_rows = {n: put(f"b{n}_row", [P, D]) for n in ("k", "v", "o")}
        bq_col = put("bq_col", [P, NG])
        den = put("den", [P, H])
        rden = put("rden", [P, H])
        assert put.at <= context_base
        put = Shelf(q_t_at)
        w_raw = {"v": put("wv_raw", [P, NC, D]), "q": put("wq_raw", [P, NC, D])}
        xw_raw = {"k": k_half, "v": Shelf(v_half_at)("xwv_raw", [P, NC, D])}

        def split(hi, lo, src, *ready):
            act.wait(*ready)
            rounded = act.run(S.activation, hi, src, ACT.Copy)
            dve.wait(rounded, *ready)
            return dve.run(V.tensor_tensor, lo, src, hi.bitcast(F32), ALU.subtract)

        def three_passes(left, right):
            return [(a, b_) for c in range(NC) for a, b_ in ((left[0][:, c], right[0][:, c]),
                                                             (left[0][:, c], right[1][:, c]),
                                                             (left[1][:, c], right[0][:, c]))]

        def columns(parts, cols):
            return [part[:, :, cols] for part in parts]

        def transpose_tile(i, row):
            for c in range(NC):
                issue = pe.run if c == NC - 1 else pe.quiet
                done = issue(nc.tensor.transpose, bank(i)[:, c * P:(c + 1) * P], row[:, c * P:(c + 1) * P],
                             identity[:, :])
            return done

        class Ring:

            def __init__(self, *banks):
                self.banks, self.turn = banks, 0

            def __call__(self):
                i = self.banks[self.turn % len(self.banks)]
                self.turn += 1
                pe.wait(bank_free[i])
                return i

        def together(main, main_units, beside, beside_units, first=0):
            done = 0
            for i, _ in enumerate(main):
                while done < beside_units * (i + 1 - first) // (main_units - first):
                    next(beside, None)
                    done += 1
            for _ in beside:
                pass

        def snapshot():
            return [x.last() for x in engines] + [s.all() for s in streams]

        main_bank, side_bank = Ring(0, 1, 2, 3), Ring(4, 5, 6, 7)
        raw_in, part_out, v_out = streams_of("raw_in", 2), streams_of("part_out", 2), streams_of("v_out", 2)
        x_in, x1_out = streams_of("x_in", NH), streams_of("x1_out", NH)
        w_in = {n: stream(f"w{n}_in") for n in ("k", "v", "q", "o", "xq")}
        bias_in = stream("bias_in")
        MCH = M // HALF
        chunks = [t["x_t"][b][:, h * HALF:(h + 1) * HALF] for b in range(B) for h in range(NH)] + \
                 [t["ctx_t"][b][:, c * HALF:(c + 1) * HALF] for b in range(B) for c in range(MCH)]
        raw_ready, raw_free, chunk_ready, chunk_used = {}, [None, None], {}, {}

        def load_chunk(m):
            if m < len(chunks):
                sp.wait(raw_free[m % 2])
                raw_ready[m] = sp.dma(raw_in[m % 2], raw[m % 2][:, :, :], chunks[m].rearrange("(c p) n -> p c n", p=P))

        def split_chunk(m, c):
            if m < len(chunks):
                hi, lo = src_parts[m % 2]
                chunk_ready[m] = raw_free[m % 2] = split(hi[:, c, :], lo[:, c, :], raw[m % 2][:, c, :],
                                                         raw_ready[m], chunk_used.get(m - 2))

        w_raw["k"] = raw[1]
        w_loaded, w_ready, w_used = {}, {}, {}

        def load_weight(name, src, tile, *free):
            sp.wait(*free)
            w_loaded[name] = sp.dma(w_in[name], tile[:, :, :], t[src].rearrange("(c p) n -> p c n", p=P))

        def split_weight(name, source, c):
            hi, lo = w_parts[name]
            w_ready[name] = split(hi[:, c, :], lo[:, c, :], source[:, c, :], w_loaded[name], w_used.get(name))

        load_chunk(0)
        load_weight("k", "wk_t", w_raw["k"])
        load_weight("v", "wv_t", w_raw["v"])
        for n in ("k", "v", "o"):
            sp.dma(bias_in, bias_rows[n][:, :], t[f"L0_attn_b{n}"].partition_broadcast(P))
        bias_ready = sp.dma(bias_in, bq_col[:, :], t["bq_cols"])
        load_weight("q", "wq_t", w_raw["q"])
        ones_set = dve.run(V.memset, v_half[:, :, :, P:P + 1], 1.0)
        for c in range(NC):
            split_chunk(0, c)
            split_weight("k", w_raw["k"], c)
        raw_free[1] = w_ready["k"]
        load_chunk(1)
        load_weight("o", "wo_t", wo)
        load_weight("xq", "xwq_t", wxq)
        dve.wait(bias_ready)
        act.wait(bias_ready)

        x_ready, x_used = {}, {}

        def fetch_x(b, h):
            if b < B:
                sp.wait(x1_out[h].all(), x_used.get(h))
                loaded = sp.dma(x_in[h], x_nat[h][:, :, :], t["x"][b][h * HALF:(h + 1) * HALF, :]
                                .rearrange("(n p) d -> p n d", p=P))
                pool.wait(loaded, bias_ready)
                for k in range(HT):
                    x_ready[b, h] = pool.run(G.tensor_tensor, x_nat[h][:, k, :], x_nat[h][:, k, :],
                                             bias_rows["o"][:, :], ALU.add)

        fetch_x(0, 0)
        fetch_x(0, 1)

        parts_turn = 0

        def store_parts(i, done, dest):
            nonlocal parts_turn
            s = parts_turn % 2
            parts_turn += 1
            hi, lo = out_parts[s]
            bank_free[i] = stored = split(hi[:, :], lo[:, :], bank(i), done, part_out[s].all())
            sp.wait(stored)
            for part, tile in enumerate((hi, lo)):
                sp.dma(part_out[s], dest[:, part], tile[:, :].bitcast(F32))

        low_free = [None, None]
        kv_used = [None]
        keys_used = [None]
        q_used = {}
        kv_ready, queries_ready = {}, {}

        def linear_attention_sums(b):
            for h in range(NH):
                m = b * NH + h
                src = src_parts[m % 2]
                load_chunk(m + 2)
                pe.wait(chunk_ready[m])
                for n in range(HT):
                    x_tile = columns(src, slice(n * P, (n + 1) * P))
                    pe.wait(w_ready["k"])
                    i = main_bank()
                    done = w_used["k"] = accumulate(bank(i), three_passes(x_tile, w_parts["k"]))
                    s = n % 2
                    dve.wait(done, low_free[s])
                    a = bank_free[i] = dve.run(V.tensor_tensor, pre[s][:, :], bank(i), bias_rows["k"][:, :], ALU.add)
                    below = dve.then(V.tensor_scalar, low[s][:, :], pre[s][:, :], 0.0, None, ALU.min)
                    act.wait(below)
                    exp_done = act.run(S.activation, low[s][:, :], low[s][:, :], ACT.Exp)
                    if m == 0 and n == 0:
                        for c in range(NC):
                            split_weight("v", w_raw["v"], c)
                    yield
                    pe.wait(w_ready["v"])
                    i = main_bank()
                    done = w_used["v"] = accumulate(bank(i), three_passes(x_tile, w_parts["v"]))
                    dve.wait(done, keys_used[0])
                    bank_free[i] = dve.run(V.tensor_tensor, v_half[:, n, :, 0:P],
                                           bank(i).rearrange("p (g e) -> p g e", g=NG),
                                           bias_rows["v"][:, :].rearrange("p (g e) -> p g e", g=NG), ALU.add)
                    dve.wait(exp_done)
                    keys_ready = low_free[s] = dve.run(V.scalar_tensor_tensor, k_half[:, n, :], pre[s][:, :], 0.0,
                                                       low[s][:, :], ALU.max, ALU.add)
                    if m == 0 and n == 1:
                        for c in range(NC):
                            split_weight("q", w_raw["q"], c)
                    split_chunk(m + 1, n)
                    yield
                for g in range(NG):
                    s = g % 2
                    pe.wait(w_ready["q"])
                    i = main_bank()
                    done = chunk_used[m] = accumulate(
                        bank(i), three_passes(columns(w_parts["q"], slice(g * P, (g + 1) * P)), src))
                    dve.wait(done, low_free[s])
                    below = dve.run(V.tensor_scalar, low[s][:, :], bank(i), bq_col[:, g:g + 1], 0.0, ALU.add, ALU.min)
                    act.wait(below)
                    act.run(S.activation, low[s][:, :], low[s][:, :], ACT.Exp)
                    above = bank_free[i] = act.run(S.activation, pre[s][:, :], bank(i), ACT.Relu,
                                                   bias=bq_col[:, g:g + 1])
                    dve.wait(above, q_used.get(h), w_ready["q"])
                    queries_ready[b, h] = low_free[s] = dve.run(V.tensor_tensor, q_t[:, g, h * HALF:(h + 1) * HALF],
                                                            pre[s][:, :], low[s][:, :], ALU.add)
                    yield
                    if g == 0:
                        pe.wait(keys_ready, ones_set)
                        for gg in range(NG):
                            i = main_bank()
                            done = keys_used[0] = accumulate(
                                bank(i)[:, 0:P + 1], [(k_half[:, n, gg * P:(gg + 1) * P], v_half[:, n, gg, :])
                                                      for n in range(HT)])
                            dve.wait(done)
                            if h == 0:
                                bank_free[i] = dve.run(V.tensor_copy, kv_part[:, gg, :], bank(i)[:, 0:P + 1])
                            else:
                                bank_free[i] = dve.run(V.tensor_tensor, kv_part[:, gg, :], bank(i)[:, 0:P + 1],
                                                       kv_part[:, gg, :], ALU.add)
                        if h == NH - 1:
                            dve.wait(bank_free[i], kv_used[0], const_in.all())
                            for gg in range(NG):
                                dve.run(V.tensor_tensor, kv[:, gg, 0:P], kv_part[:, gg, 0:P], same_head[:, :], ALU.mult)
                                kv_ready[b] = dve.run(V.tensor_scalar, kv[:, gg, P:P + HG], head_of[:, :],
                                                      kv_part[:, gg, P:P + 1], None, ALU.mult)
                        if m == B * NH - 1:
                            load_weight("k", "xwk_t", xw_raw["k"], keys_used[0])
                            load_weight("v", "xwv_t", xw_raw["v"], keys_used[0])
                        yield
                    elif m == B * NH - 1:
                        for c in range(NC):
                            if g < NG - 1:
                                name = ("k", "v")[g - 1]
                                split_weight(name, xw_raw[name], c)

        SUM_UNITS = NH * (2 * HT + NG + 1)

        def attention_rows(b):
            att_ready, att_used, att_t_ready, att_t_used = {}, {}, {}, [None]
            x1_ready, x1_t_ready = {}, {}

            def heads_of_tile(n):
                pe.wait(kv_ready[b], queries_ready[b, n // HT])
                dve.wait(att_used.get(n - 2))
                for pair in range(NG // 2):
                    i = side_bank()
                    for k in range(2):
                        g = 2 * pair + k
                        done = accumulate(bank(i)[:, k * (P + HG):(k + 1) * (P + HG)],
                                          [(q_t[:, g, n * P:(n + 1) * P], kv[:, g, :])])
                    both = bank(i)[:, 0:2 * (P + HG)].rearrange("p (k w) -> p k w", k=2)
                    hs = slice(pair * 2 * HG, (pair + 1) * 2 * HG)
                    dve.wait(done)
                    dve.run(V.tensor_scalar, den[:, hs].rearrange("p (k h) -> p k h", k=2),
                            both[:, :, P:P + HG], 1e-6, None, ALU.max)
                    dve.then(V.reciprocal, rden[:, hs], den[:, hs])
                    dve.wait(dve.last())
                    for k in range(2):
                        g = 2 * pair + k
                        bank_free[i] = att_ready[n] = dve.run(
                            V.tensor_tensor, att[n % 2][:, g * P:(g + 1) * P].rearrange("p (h e) -> p h e", h=HG),
                            both[:, k, 0:P].rearrange("p (h e) -> p h e", h=HG),
                            rden[:, g * HG:(g + 1) * HG].unsqueeze(2).to_broadcast([P, HG, DH]), ALU.mult)
                q_used[n // HT] = kv_used[0] = done

            def transpose_heads(n):
                pe.wait(att_ready[n], const_in.all())
                i = side_bank()
                done = att_used[n] = transpose_tile(i, att[n % 2])
                act.wait(done, att_t_used[0])
                att_t_ready[n] = bank_free[i] = act.run(
                    S.activation, att_t[:, :, :].rearrange("p g n -> p (g n)"), bank(i), ACT.Copy)

            def project(n):
                rows = x_nat[n // HT][:, n % HT, :]
                pe.wait(att_t_ready[n], w_loaded["o"])
                i = side_bank()
                done = att_t_used[0] = accumulate(bank(i), [(att_t[:, g, :], wo[:, g, :]) for g in range(NG)])
                dve.wait(done, x_ready[b, n // HT])
                bank_free[i] = dve.run(V.tensor_tensor, rows, bank(i), rows, ALU.add)
                tile_statistics(rows, n % HT)

            def stage(n):
                if 2 <= n:
                    project(n - 2)
                if 1 <= n <= NT:
                    transpose_heads(n - 1)
                if n < NT:
                    heads_of_tile(n)

            def layernorm(h):
                dve.wait(rsqrt_of_variances(HT))
                for k in range(HT):
                    x1_ready[h] = normalise(x_nat[h][:, k, :], x_nat[h][:, k, :], k)
                sp.wait(x1_ready[h])
                first = b * T + h * HALF
                sp.dma(x1_out[h], x1_rows[first:first + HALF, :].rearrange("(n p) d -> p n d", p=P), x_nat[h][:, :, :])

            def transpose_x1(h, k):
                for k in (k, k + 1):
                    pe.wait(x1_ready[h])
                    i = side_bank()
                    done = x_used[h] = transpose_tile(i, x_nat[h][:, k, :])
                    act.wait(done, x1_t_used[0])
                    x1_t_ready[h] = bank_free[i] = act.run(S.activation, x1_t[:, :, k * P:(k + 1) * P],
                                                           bank(i).rearrange("p (c n) -> p c n", c=NC), ACT.Copy)

            def queries(h, g):
                pe.wait(x1_t_ready[h], w_loaded["xq"])
                i = side_bank()
                done = x1_t_used[0] = accumulate(bank(i), [(wxq[:, c, g * P:(g + 1) * P], x1_t[:, c, :])
                                                           for c in range(NC)])
                store_parts(i, done, q_parts[b, g * HG:(g + 1) * HG, :, :, h * HALF:(h + 1) * HALF])

            for n in range(HT + 2):
                stage(n)
                yield
            layernorm(0)
            stage(HT + 2)
            yield
            transpose_x1(0, 0)
            stage(HT + 3)
            yield
            transpose_x1(0, 2)
            fetch_x(b + 1, 0)
            stage(HT + 4)
            yield
            queries(0, 0)
            stage(HT + 5)
            yield
            layernorm(1)
            for g in range(1, NG):
                queries(0, g)
                yield
            for k in (0, 2):
                transpose_x1(1, k)
                yield
            fetch_x(b + 1, 1)
            for g in range(NG):
                queries(1, g)
                yield

        x1_t_used = [None]
        ROW_UNITS = NT + 2 + NG - 1 + 2 + NG

        def context(b):
            for mc in range(MCH):
                m = B * NH + b * MCH + mc
                src = src_parts[m % 2]
                load_chunk(m + 2)
                pe.wait(chunk_ready[m], w_ready["k"], w_ready["v"])
                for u in range(NG):
                    i = main_bank()
                    done = accumulate(bank(i), three_passes(columns(w_parts["k"], slice(u * P, (u + 1) * P)), src))
                    store_parts(i, done, k_parts[b, u * HG:(u + 1) * HG, :, :, mc * HALF:(mc + 1) * HALF])
                    yield
                    s = u % 2
                    i = main_bank()
                    done = chunk_used[m] = accumulate(
                        bank(i), three_passes(columns(src, slice(u * P, (u + 1) * P)), w_parts["v"]))
                    act.wait(done, v_out[s].all(), low_free[s])
                    copied = bank_free[i] = act.run(S.activation, pre[s][:, :], bank(i), ACT.Copy)
                    sp.wait(copied)
                    sp.dma(v_out[s], v_rows[b, :, :, mc * HT + u, :].rearrange("g p e -> p g e"),
                           pre[s][:, :].rearrange("p (g e) -> p g e", g=NG))
                    split_chunk(m + 1, u)
                    yield

        CONTEXT_UNITS = MCH * 2 * NG
        assert HT == NC == NG == HALF // P

        for _ in linear_attention_sums(0):
            pass
        together(linear_attention_sums(1), SUM_UNITS, attention_rows(0), ROW_UNITS)
        together(context(0), CONTEXT_UNITS, attention_rows(1), ROW_UNITS)
        attention_end = snapshot()

        x2_out, table_out = streams_of("x2_out", NH), streams_of("table_out", TABLES)
        if True:
            groups = [(b, g) for b in range(B) for g in range(NG)]
            KCH = M // HALF
            k_in = [streams_of(f"k_in{i}_", KCH) for i in range(2)]
            q_in = [streams_of(f"q_in{i}_", NH) for i in range(2)]
            shift_in = streams_of("shift_in", 2)
            v_in = streams_of("v_in", 2)
            xwo_in, y_in = stream("xwo_in"), streams_of("y_in", NH)
            k_ready, q_ready, v_ready, shift_ready = {}, {}, {}, {}

            def load_k(n, c, free=None):
                if n >= len(groups):
                    return
                b, g = groups[n]
                src = k_parts[b, g * HG:(g + 1) * HG, :, :, c * HALF:(c + 1) * HALF]
                dst = k_stack[n % 2][:, :, c * HALF:(c + 1) * HALF].bitcast(F32)
                sp.wait(free)
                sp.dma(k_in[n % 2][c], dst[0:2 * DH], src.rearrange("j l r m -> (l r) j m"))
                k_ready[n, c] = sp.dma(k_in[n % 2][c], dst[2 * DH:STK], src[:, 0].rearrange("j r m -> r j m"))

            def load_q(n, h, free=None):
                if n >= len(groups):
                    return
                b, g = groups[n]
                src = q_parts[b, g * HG:(g + 1) * HG, :, :, h * HALF:(h + 1) * HALF]
                dst = q_stack[n % 2][:, :, h * HALF:(h + 1) * HALF].bitcast(F32)
                sp.wait(free)
                sp.dma(q_in[n % 2][h], dst[0:DH], src[:, 0].rearrange("j r m -> r j m"))
                q_ready[n, h] = sp.dma(q_in[n % 2][h], dst[DH:STK], src.rearrange("j l r m -> (l r) j m"))

            def load_v(n, free=None):
                if n >= len(groups):
                    return
                b, g = groups[n]
                sp.wait(free)
                v_ready[n] = sp.dma(v_in[n % 2], v_grp[n % 2][:, :, :], v_rows[b, g])

            NUM, DEN = 6, 7

            next_score_bank, next_s_bank = Ring(0, 1, 2), Ring(3, 4, 5)

            def max_pass(n, ring):
                ks, qs = k_stack[n % 2], q_stack[n % 2]
                for mc in range(KCH):
                    pe.wait(k_ready[n, mc])
                    for nt in range(NT):
                        pe.wait(q_ready[n, nt * P // HALF])
                        for j in range(HG):
                            i = ring()
                            done = accumulate(bank(i), [(qs[0:STK, j, nt * P:(nt + 1) * P],
                                                         ks[0:STK, j, mc * HALF:(mc + 1) * HALF])])
                            dve.wait(done)
                            bank_free[i] = dve.run(V.reduce_max, max4[:, nt, j, mc:mc + 1], bank(i), AX.X)
                            yield

            shift_taken = [None]

            def shift_pass(n):
                dve.wait(shift_taken[0])
                dve.then(V.tensor_reduce, neg_max[:, :, :], max4[:, :, :, :], AX.X, ALU.max)
                dve.then(V.tensor_scalar, neg_max[:, :, :], neg_max[:, :, :], -1.0, None, ALU.mult)
                dve.then(V.tensor_copy, max_hi[:, :, :], neg_max[:, :, :])
                dve.then(V.tensor_copy, max_parts[:, :, 0, :], max_hi[:, :, :].bitcast(F32))
                parts_ready = dve.then(V.tensor_tensor, max_parts[:, :, 1, :], neg_max[:, :, :],
                                       max_hi[:, :, :].bitcast(F32), ALU.subtract)
                pe.wait(parts_ready)
                for h in range(NH):
                    i = next_s_bank()
                    for q in range(HALF // P):
                        nt = h * (HALF // P) + q
                        done = accumulate(bank(i)[0:SHIFT * HG, q * P:(q + 1) * P],
                                          [(max_parts[:, nt, :, :].rearrange("p l j -> p (l j)"), identity[:, :])])
                    act.wait(done, shift_in[(n - 1) % 2].all())
                    rows = bank_free[i] = act.run(S.activation, shift_rows[:, h * HALF:(h + 1) * HALF],
                                                  bank(i)[0:SHIFT * HG, :], ACT.Copy)
                shift_taken[0] = done
                sp.wait(rows, q_free[n % 2])
                for part in range(SHIFT):
                    shift_ready[n] = sp.dma(shift_in[n % 2], q_stack[n % 2][STK + part:STK + part + 1, :, :].bitcast(F32),
                                            shift_rows[part * HG:(part + 1) * HG, :].bitcast(F32))

            q_free = [None, None]
            probs_free = [None] * NP
            probs_turn = 0
            heads_free, heads_ready, rows_used = [None] * NH, [None] * NH, {}

            def open_group(n):
                for h in range(NH):
                    load_q(n, h)
                for c in range(KCH):
                    load_k(n, c)
                load_v(n)

            def one_rows(n):
                pe.wait(dve.run(V.memset, k_stack[n][STK:STK + SHIFT, :, :].bitcast(F32), 1.0))

            sp.wait(*attention_end)
            open_group(0)
            together(context(1), CONTEXT_UNITS, max_pass(0, side_bank), KCH * NT * HG, first=NG)
            for engine in (dve, act, pool):
                engine.wait(*attention_end)
            one_rows(0)
            shift_pass(0)
            context_end = snapshot()

            rows_ready = {}

            def fetch_rows(b, hh):
                ys = y_nat[hh]
                sp.wait(x2_out[hh].all(), rows_used.get(hh))
                y_ready = sp.dma(y_in[hh], ys[:, :, :], x1_rows[(b * NT + hh * HT) * P:(b * NT + (hh + 1) * HT) * P, :]
                                 .rearrange("(n p) d -> p n d", p=P))
                pool.wait(y_ready, xwo_ready)
                for k in range(HT):
                    rows_ready[b, hh] = pool.run(G.tensor_tensor, ys[:, k, :], ys[:, k, :], xbo_row[:, :], ALU.add)

            def rows_of(b, hh):
                ys = y_nat[hh]
                pe.wait(heads_ready[hh], xwo_ready)
                for k in range(HT):
                    n = hh * HT + k
                    i = next_s_bank()
                    done = accumulate(bank(i), [(heads_t[:, g, n * P:(n + 1) * P], xwo[:, g, :])
                                                for g in range(NG)])
                    dve.wait(done, rows_ready[b, hh])
                    bank_free[i] = dve.run(V.tensor_tensor, ys[:, k, :], bank(i), ys[:, k, :], ALU.add)
                    tile_statistics(ys[:, k, :], k)
                    yield
                heads_free[hh] = done
                dve.wait(rsqrt_of_variances(HT))
                x2_ready = [normalise(ys[:, k, :], ys[:, k, :], k) for k in range(HT)]
                sp.wait(x2_ready[-1])
                first = (b * NT + hh * HT) * P
                for rows in (x2_rows, y_rows):
                    sp.dma(x2_out[hh], rows[first:first + HT * P, :].rearrange("(n p) d -> p n d", p=P), ys[:, :, :])
                yield
                x2_t_ready, x2_t_free = [None] * HT, [None] * HT

                def transpose_rows(k):
                    pe.wait(x2_ready[k])
                    i = next_s_bank()
                    for c in range(NC):
                        issue = pe.run if c == NC - 1 else pe.quiet
                        done = issue(nc.tensor.transpose, bank(i)[:, c * P:(c + 1) * P],
                                     ys[:, k, c * P:(c + 1) * P], identity[:, :])
                    rows_used[hh] = done
                    act.wait(done, x2_t_free[k - 2] if k >= 2 else None)
                    x2_t_ready[k] = bank_free[i] = act.run(
                        S.activation, x2_t[k % 2][:, :, :].rearrange("p c n -> p (c n)"), bank(i), ACT.Copy)

                def logits(k):
                    pe.wait(x2_t_ready[k])
                    i = next_s_bank()
                    x2_t_free[k] = done = accumulate(bank(i)[:, 0:E], [(x2_t[k % 2][:, c, :], router_w[:, c, :])
                                                                      for c in range(NC)])
                    dve.wait(done)
                    bank_free[i] = dve.run(V.tensor_tensor, lg[:, k, :], bank(i)[:, 0:E], router_bias[:, :], ALU.add)

                transpose_rows(0)
                transpose_rows(1)
                yield
                for k in range(HT):
                    logits(k)
                    if k + 2 < HT:
                        transpose_rows(k + 2)
                    yield

                def per_tile(x):
                    return x[:, :].unsqueeze(2).to_broadcast([P, HT, E])

                def per_expert(x):
                    return x[:, :].unsqueeze(1).to_broadcast([P, HT, E])

                def third(x, k):
                    return x[:, :, k:k + 1].to_broadcast([P, HT, E])

                dve.then(V.reduce_max, col["max"][:, :], lg[:, :, :], AX.X)
                lg_ready = dve.then(V.tensor_tensor, lg[:, :, :], lg[:, :, :], per_tile(col["max"]), ALU.subtract)
                act.wait(lg_ready)
                ex_ready = act.run(S.activation, ex8[:, :, :], lg[:, :, :], ACT.Exp)
                yield
                dve.wait(ex_ready)
                dve.then(V.reduce_sum, col["sum"][:, :], ex8[:, :, :], AX.X)
                dve.then(V.reciprocal, col["r"][:, :], col["sum"][:, :])
                dve.wait(dve.then(V.tensor_tensor, pr[:, :, :], ex8[:, :, :], per_tile(col["r"]), ALU.mult))
                for k in range(HT):
                    top_done = dve.run(V.max, top8[:, k, :], pr[:, k, :])
                dve.wait(top_done)
                for k in range(HT):
                    dve.run(V.max_index, idx8[:, k, :], top8[:, k, :], pr[:, k, :])
                dve.then(V.tensor_copy, idxf[:, :, :], idx8[:, :, :])
                dve.then(V.tensor_tensor, oh0[:, :, :], per_expert(expert_no), third(idxf, 0), ALU.is_equal)
                dve.then(V.tensor_tensor, oh1[:, :, :], per_expert(expert_no), third(idxf, 1), ALU.is_equal)
                dve.then(V.tensor_tensor, ms[:, :, :], oh0[:, :, :], oh1[:, :, :], ALU.add)
                dve.then(V.tensor_copy, before[:, 0, :], before[:, HT, :])
                for k in range(HT):
                    before_ready = dve.then(V.tensor_tensor, before[:, k + 1, :], before[:, k, :], ms[:, k, :],
                                            ALU.add)
                yield
                pe.wait(before_ready)
                i = next_s_bank()
                for k in range(HT):
                    ranks_done = accumulate(bank(i)[:, k * E:(k + 1) * E],
                                            [(earlier[:, :], ms[:, k, :]), (ones[:, :], before[:, k, :])])
                rank = bank(i)[:, 0:HT * E].rearrange("p (n e) -> p n e", n=HT)
                dve.then(V.tensor_tensor, col["s"][:, :], top8[:, :, 0], top8[:, :, 1], ALU.add)
                dve.then(V.tensor_scalar, col["s"][:, :], col["s"][:, :], 1e-9, None, ALU.max)
                dve.then(V.reciprocal, col["r"][:, :], col["s"][:, :])
                dve.wait(ranks_done)
                dve.run(V.tensor_scalar, kp[:, :, :], rank, float(CAP), None, ALU.is_lt)
                bank_free[i] = dve.then(V.tensor_tensor, sv[:, :, :], rank, per_expert(expert_base), ALU.add)
                tiles = slice(b * NT + hh * HT, b * NT + (hh + 1) * HT)
                for k, oh in enumerate((oh0, oh1)):
                    dve.then(V.tensor_tensor, picked[:, :, :], oh[:, :, :], sv[:, :, :], ALU.mult)
                    dve.then(V.reduce_sum, col["slot"][:, :], picked[:, :, :], AX.X)
                    dve.then(V.tensor_tensor, picked[:, :, :], oh[:, :, :], kp[:, :, :], ALU.mult)
                    dve.then(V.reduce_sum, col["k"][:, :], picked[:, :, :], AX.X)
                    dve.then(V.tensor_scalar, col["slot"][:, :], col["slot"][:, :], dump_slot[:, :], None,
                             ALU.subtract)
                    dve.then(V.tensor_tensor, col["slot"][:, :], col["slot"][:, :], col["k"][:, :], ALU.mult)
                    dve.then(V.tensor_scalar, col["slot"][:, :], col["slot"][:, :], dump_slot[:, :], None, ALU.add)
                    dve.then(V.tensor_copy, slot_i[:, tiles, k], col["slot"][:, :])
                    dve.run(V.tensor_tensor, entry[:, tiles, k, 1], top8[:, :, k], col["r"][:, :], ALU.mult)
                    entry_ready = dve.run(V.tensor_copy, entry[:, tiles, k, 0], token_no[:, tiles])
                pool.wait(entry_ready, scratch_init.all())
                for n in range(tiles.start, tiles.stop):
                    for k in range(TOPK):
                        which = (n % 2) * TOPK + k
                        pool.wait(table_out[which].all())
                        pool.indirect(table_out[which], out=slot_tables[which],
                                      out_offset=bass.IndirectOffsetOnAxis(ap=slot_i[:, n, k:k + 1], axis=0),
                                      in_=entry[:, n, k, :], in_offset=None)
                yield

            sides = []

            def side():
                while sides:
                    try:
                        next(sides[0])
                        return
                    except StopIteration:
                        sides.pop(0)

            divisions = []
            PIECE = HALF // 8

            def divide(pieces):
                nonlocal divided
                for _ in range(min(pieces, len(divisions))):
                    copied, b, g, h, q = divisions.pop(0)
                    dve.wait(copied, heads_free[h])
                    cols = slice(q * PIECE, (q + 1) * PIECE)
                    dve.run(V.reciprocal, den_c[:, cols], den_c[:, cols])
                    divided = heads_ready[h] = dve.then(V.tensor_tensor, heads_t[:, g, h * HALF + q * PIECE:h * HALF + (q + 1) * PIECE],
                                           num_c[:, cols], den_c[:, cols], ALU.mult)
                    if g == NG - 1 and q == HALF // PIECE - 1:
                        sides.append(rows_of(b, h))

            pending = []
            clock = 0

            def denominators(until):
                while pending and pending[0][0] <= until:
                    _, q, summed, mt, b, g, h = pending.pop(0)
                    pe.wait(summed)
                    if mt == 1:
                        pe.wait(bank_free[DEN])
                    for j in range(HG):
                        den_done = accumulate(bank(DEN)[j * DH:(j + 1) * DH, :],
                                              [(ones[:, 0:DH], probs[q][:, j, :])],
                                              start=mt == 1, stop=mt == MT - 1)
                    probs_free[q] = (den_done,)
                    if mt == MT - 1:
                        act.wait(den_done, divided)
                        bank_free[DEN] = copied = act.run(S.activation, den_c[:, :], bank(DEN), ACT.Copy)
                        divisions.extend((copied, b, g, h, q) for q in range(HALF // PIECE))

            divided = None
            for n, (b, g) in enumerate(groups):
                if n == 1:
                    one_rows(1)
                ks, qs, vs = k_stack[n % 2], q_stack[n % 2], v_grp[n % 2]
                ahead = max_pass(n + 1, next_s_bank) if n + 1 < len(groups) else None
                todo = KCH * NT * HG if ahead else 0
                steps = [(h, mt) for h in range(NH) for mt in range(MT)]
                FIRST, LAST = (0 if n else 4), 28
                issued = 0
                allowed = 0

                def maxima(count=1):
                    nonlocal issued, ahead
                    while ahead and count and issued < allowed:
                        next(ahead)
                        issued += 1
                        count -= 1
                    if ahead and issued == todo:
                        for _ in ahead:
                            pass
                        shift_pass(n + 1)
                        ahead = None

                def scores(h, mt, p, heads):
                    pe.wait(k_ready[n, mt * P // HALF], q_ready[n, h], shift_ready[n])
                    act.wait(*(probs_free[p] or ()))
                    for j in heads:
                        i = next_score_bank()
                        done = accumulate(bank(i), [(ks[0:STK + SHIFT, j, mt * P:(mt + 1) * P],
                                                     qs[0:STK + SHIFT, j, h * HALF:(h + 1) * HALF])])
                        act.wait(done)
                        exp_done = bank_free[i] = act.run(S.activation, probs[p][:, j, :], bank(i), ACT.Exp,
                                                          scale=SCALE)
                    maxima()
                    return p, exp_done, done

                def next_probs():
                    nonlocal probs_turn
                    probs_turn += 1
                    return (probs_turn - 1) % NP

                current = scores(*steps[0], next_probs(), range(HG))
                for s, (h, mt) in enumerate(steps):
                    p, exp_done, _ = current
                    denominators(clock)
                    maxima()
                    if ahead:
                        allowed = max(0, min(todo, -(-todo * (s + 1 - FIRST) // (LAST - FIRST))))
                    if n == 0 and s == 1:
                        for engine in (sp, act, dve, pool):
                            engine.wait(*context_end)
                        open_group(1)
                        sp.dma(xwo_in, xwo[:, :, :], t["xwo_t"].rearrange("(c p) n -> p c n", p=P))
                        xwo_ready = sp.dma(xwo_in, xbo_row[:, :], t["L0_xattn_bo"].partition_broadcast(P))
                        dve.run(V.memset, before[:, :, :], 0.0)
                    if s + 1 < len(steps):
                        p_next = next_probs()
                        scores(*steps[s + 1], p_next, range(HG // 2))
                    pe.wait(exp_done, v_ready[n])
                    if mt == 0:
                        pe.wait(bank_free[NUM])
                    for j in range(HG):
                        num_done = accumulate(bank(NUM)[j * DH:(j + 1) * DH, :],
                                              [(vs[:, mt, j * DH:(j + 1) * DH], probs[p][:, j, :])],
                                              start=mt == 0, stop=mt == MT - 1)
                    maxima()
                    if s + 1 < len(steps):
                        following = scores(*steps[s + 1], p_next, range(HG // 2, HG))
                        h2, mt2 = steps[s + 1]
                        if h2 == NH - 1 and mt2 % (HALF // P) == HALF // P - 1:
                            load_k(n + 2, mt2 * P // HALF, following[2])
                    if s == MT - 1:
                        load_q(n + 2, 0, following[2])
                    if mt % 2 == 0:
                        even = p, num_done
                    else:
                        pool.wait(exp_done, even[1])
                        summed = pool.run(G.tensor_tensor, probs[even[0]][:, :, :], probs[even[0]][:, :, :],
                                          probs[p][:, :, :], ALU.add)
                        probs_free[p] = (num_done, summed)
                        pending.append((clock + 2, even[0], summed, mt, b, g, h))
                    maxima(2)
                    divide(2)
                    side()
                    if n == len(groups) - 1:
                        side()
                    if g == NG - 1 and mt == 2:
                        fetch_rows(b, h)
                    if mt == MT - 1:
                        divide(len(divisions))
                        act.wait(num_done, divided)
                        bank_free[NUM] = act.run(S.activation, num_c[:, :], bank(NUM), ACT.Copy)
                    clock += 1
                    current = following
                q_free[n % 2] = current[2]
                load_q(n + 2, 1, current[2])
                load_v(n + 2, num_done)
                if n == len(groups) - 1:
                    denominators(clock + 3)
                    loop_end = [x.last() for x in engines]
                    divide(len(divisions))

        y_add, out_done = stream("y_add"), streams_of("out_done", 2)
        put = Shelf(loop_base)
        w1_raw = put("w1_raw", [P, NC, F])
        w2_raw = put("w2_raw", [P, NF, D])
        w1_hi, w1_lo = (put(f"w1_{n}", [P, NC, F], F32R) for n in ("hi", "lo"))
        w2_hi, w2_lo = (put(f"w2_{n}", [P, NF, D], F32R) for n in ("hi", "lo"))
        xe_hi, xe_lo = (put(f"xe_{n}", [P, NC, CAP], F32R) for n in ("hi", "lo"))
        hid_hi = put("hid_hi", [P, NF, CAP], F32R)
        xg = [put(f"xg{i}", [P, D]) for i in range(NS)]
        assert put.at <= tail_base
        put = Shelf(tail_base)
        hid_lo = put("hid_lo", [P, NF, CAP], F32R)
        hid = [put(f"hid{i}", [P, CAP]) for i in range(2)]
        eo = [put(f"eo{i}", [P, D]) for i in range(3)]
        b2s = [put(f"b2s{i}", [P, D]) for i in range(2)]
        w1_in, w2_in, b2_in = stream("w1_in"), stream("w2_in"), streams_of("b2_in", 2)
        b1_in, table_in = stream("b1_in"), streams_of("table_in", TABLES)
        xg_in = streams_of("xg_in", NS)

        raw_ready, split_ready, raw_free = {}, {}, {}

        def fetch_w1(e):
            if e < E:
                sp.wait(raw_free.get(1))
                raw_ready[e, 1] = sp.dma(w1_in, w1_raw[:, :, :],
                                         t["L0_ffn_w1"][e].rearrange("(c p) f -> p c f", p=P))

        def fetch_w2(e):
            if e < E:
                sp.wait(raw_free.get(2))
                raw_ready[e, 2] = sp.dma(w2_in, w2_raw[:, :, :],
                                         t["L0_ffn_w2"][e].rearrange("(c p) d -> p c d", p=P))

        def split_w1(e, c, used):
            if e < E:
                dve.wait(used)
                split_ready[e, 1] = raw_free[1] = split(w1_hi[:, c, :], w1_lo[:, c, :], w1_raw[:, c, :],
                                                        used, raw_ready[e, 1])

        def split_w2(e, f, used):
            if e < E:
                dve.wait(used)
                split_ready[e, 2] = raw_free[2] = split(w2_hi[:, f:f + 2, :], w2_lo[:, f:f + 2, :],
                                                        w2_raw[:, f:f + 2, :], used, raw_ready[e, 2])

        sp.wait(*loop_end)
        fetch_w1(0)
        fetch_w2(0)
        b1_ready = sp.dma(b1_in, b1c[:, :, :], t["b1_cols"])
        while sides:
            side()
        tail_end = [x.last() for x in engines] + [s.all() for s in x2_out]
        act.wait(*loop_end)
        dve.wait(*loop_end)
        pool.wait(*loop_end)
        for c in range(NC):
            split_w1(0, c, None)
        for f in range(0, NF, 2):
            split_w2(0, f, None)
        sp.wait(*(x.all() for x in table_out))
        for i in range(TABLES):
            sp.dma(table_in[i], table[:, i, :, :].rearrange("p (e i) w -> p e i w", e=E),
                   slot_tables[i][0:SLOTS, :].rearrange("(e p i) w -> p e i w", p=P, i=NS))
        dve.wait(*(x.all() for x in table_in))
        dve.run(V.tensor_tensor, table[:, 0], table[:, 0], table[:, 1], ALU.add)
        dve.run(V.tensor_tensor, table[:, 2], table[:, 2], table[:, 3], ALU.add)
        dve.then(V.tensor_tensor, table[:, 0], table[:, 0], table[:, 2], ALU.add)
        number, weight = table[:, 0, :, 0], table[:, 0, :, 1]
        spare = table[:, 1, :, 0]
        dve.then(V.tensor_scalar, spare, number, 0.0, empty_row[:, :], ALU.is_equal, ALU.mult)
        dve.then(V.tensor_tensor, spare, spare, number, ALU.add)
        dve.then(V.tensor_scalar, spare, spare, -1.0, None, ALU.add)
        tok_ready = dve.then(V.tensor_copy, tok[:, :], spare)
        pool.wait(tok_ready, *(x.all() for x in x2_out))
        act.wait(b1_ready)
        xg_ready, xg_free = {}, [None] * NS

        def gather(e, i):
            if e < E:
                pool.wait(xg_free[i])
                xg_ready[e, i] = pool.indirect(
                    xg_in[i], out=xg[i][:, :], out_offset=None, in_=x2_rows,
                    in_offset=bass.IndirectOffsetOnAxis(ap=tok[:, e * NS + i:e * NS + i + 1], axis=0))

        next_t_bank, next_o_bank = Ring(4, 5), Ring(6, 7)
        xe_ready = {}

        def transposes(e, i, used):
            if e >= E:
                return
            pe.wait(xg_ready[e, i])
            k = next_t_bank()
            for c in range(NC):
                issue = pe.run if c == NC - 1 else pe.quiet
                done = issue(nc.tensor.transpose, bank(k)[:, c * P:(c + 1) * P], xg[i][:, c * P:(c + 1) * P],
                             identity[:, :])
            xg_free[i] = done
            dve.wait(used)
            cols = slice(i * P, (i + 1) * P)
            xe_ready[e] = bank_free[k] = split(xe_hi[:, :, cols], xe_lo[:, :, cols],
                                               bank(k).rearrange("p (c n) -> p c n", c=NC), done, used)

        for i in range(NS):
            gather(0, i)
        for i in range(NS):
            transposes(0, i, None)
            gather(1, i)
        fetch_w1(1)
        for engine in (pool, act, dve, sp):
            engine.wait(*tail_end)
        eo_turn = 0
        eo_free, hid_free = [None] * 3, [None] * 2
        b2_ready, b2_free = {}, [None] * 2
        out_done_e = None
        HC = CAP // 2
        PARTS1 = ((w1_hi, xe_hi), (w1_hi, xe_lo), (w1_lo, xe_hi))
        PARTS2 = ((hid_hi, w2_hi), (hid_hi, w2_lo), (hid_lo, w2_hi))
        for e in range(E):
            sp.wait(b2_free[e % 2])
            b2_ready[e] = sp.dma(b2_in[e % 2], b2s[e % 2][:, :], t["L0_ffn_b2"][e].partition_broadcast(P))
            pe.wait(split_ready[e, 1], xe_ready[e])
            for f in range(NF):
                pr_ = f % 2
                pe.wait(bank_free[2 * pr_])
                terms = [(w[:, c, f * P:(f + 1) * P], x[:, c]) for c in range(NC) for w, x in PARTS1]
                for n, (w, x) in enumerate(terms):
                    for h in range(2):
                        last = n == len(terms) - 1
                        issue = pe.run if last and h else pe.quiet
                        done = issue(nc.tensor.matmul, pairs[pr_][:, h, 0:HC], w, x[:, h * HC:(h + 1) * HC],
                                     start=n == 0, stop=last)
                act.wait(done, hid_free[f % 2])
                hid_done = bank_free[2 * pr_] = bank_free[2 * pr_ + 1] = act.run(
                    S.activation, hid[f % 2][:, :].rearrange("p (h n) -> p h n", h=2), pairs[pr_][:, :, 0:HC],
                    ACT.Gelu, bias=b1c[:, e, f:f + 1])
                dve.wait(out_done_e)
                hid_ready = hid_free[f % 2] = split(hid_hi[:, f, :], hid_lo[:, f, :], hid[f % 2][:, :],
                                                    hid_done, out_done_e)
                if e and f < NF // 2:
                    split_w2(e, 2 * f, out_done_e)
            fetch_w2(e + 1)
            hidden_done = done
            pe.wait(split_ready[e, 2])
            for i in range(NS):
                transposes(e + 1, i, hidden_done)
                gather(e + 2, i)
                k = next_o_bank()
                if i == 0:
                    pe.wait(hid_ready)
                out_done_e = done = accumulate(bank(k), [(a[:, f, i * P:(i + 1) * P], w[:, f, :])
                                                         for f in range(NF) for a, w in PARTS2])
                s = eo_turn % 3
                eo_turn += 1
                dve.wait(done, b2_ready[e], eo_free[s])
                b2_free[e % 2] = bank_free[k] = dve.run(V.tensor_tensor, eo[s][:, :], bank(k), b2s[e % 2][:, :],
                                                        ALU.add)
                eo_ready = dve.then(V.tensor_scalar, eo[s][:, :], eo[s][:, :],
                                    weight[:, e * NS + i:e * NS + i + 1], None, ALU.mult)
                pool.wait(eo_ready, y_add.all())
                eo_free[s] = pool.indirect(
                    y_add, out=y_rows, in_=eo[s][:, :], in_offset=None, compute_op=ALU.add,
                    out_offset=bass.IndirectOffsetOnAxis(ap=tok[:, e * NS + i:e * NS + i + 1], axis=0))
                if i < NC:
                    split_w1(e + 1, i, hidden_done)
            fetch_w1(e + 2)
        added = y_add.all()
        join()

        with ExitStack() as scope:
            yf = Shelf(loop_base)("y_final", [P, B * NT, D])
            y_in2 = streams_of("yf_in", 4)
            Q4 = B * NT // 4
            for q in range(4):
                rows = y_rows[q * Q4 * P:(q + 1) * Q4 * P, :].rearrange("(n p) d -> p n d", p=P)
                sp.wait(added)
                sp.dma(y_in2[q], yf[:, q * Q4:(q + 1) * Q4, :], rows)
            out_flat = t["out"].rearrange("b s d -> (b s) d")
            for q in range(4):
                dve.wait(y_in2[q].all())
                for n in range(Q4):
                    dve.then(V.bn_stats, stats[:, :], yf[:, q * Q4 + n, :])
                    dve.then(V.bn_aggr, mean_var[:, n, :], stats[:, :])
                dve.wait(rsqrt_of_variances(Q4))
                for n in range(Q4):
                    done = normalise(yf[:, q * Q4 + n, :], yf[:, q * Q4 + n, :], n)
                act.wait(done)
                act.dma(out_done[q % 2], out_flat[q * Q4 * P:(q + 1) * Q4 * P, :].rearrange("(n p) d -> p n d", p=P),
                        yf[:, q * Q4:(q + 1) * Q4, :])
            act.wait(*[s.all() for s in streams])

        block = ctx.enter_context(nc.Block())

        @block.tensor
        def _(_eng):
            pe.emit()

        @block.vector
        def _(_eng):
            dve.emit()

        @block.scalar
        def _(_eng):
            act.emit()

        @block.gpsimd
        def _(_eng):
            pool.emit()

        @block.sync
        def _(_eng):
            sp.emit()


def kernel(**inputs):
    import concourse.bacc as _bacc
    from concourse.bass_utils import run_bass_kernel_spmd as _run

    arrays = {n: np.ascontiguousarray(inputs[n]) for n in (
        "x", "L0_attn_bk", "L0_attn_bv", "L0_attn_bo", "L0_xattn_bo", "L0_ffn_router_w",
        "L0_ffn_router_b", "L0_ffn_w1", "L0_ffn_w2", "L0_ffn_b2")}
    arrays["x_t"] = np.ascontiguousarray(np.transpose(inputs["x"], (0, 2, 1)))
    arrays["ctx_t"] = np.ascontiguousarray(np.transpose(inputs["ctx_1024"], (0, 2, 1)))
    arrays["bq_cols"] = np.ascontiguousarray(np.reshape(inputs["L0_attn_bq"], (NG, P)).transpose(1, 0))
    arrays["b1_cols"] = np.ascontiguousarray(np.reshape(inputs["L0_ffn_b1"], (E, NF, P)).transpose(2, 0, 1))
    for short, name in (("wq_t", "L0_attn_Wq"), ("wk_t", "L0_attn_Wk"), ("wv_t", "L0_attn_Wv"),
                        ("wo_t", "L0_attn_Wo"), ("xwq_t", "L0_xattn_wq"), ("xwk_t", "L0_xattn_wk"),
                        ("xwv_t", "L0_xattn_wv"), ("xwo_t", "L0_xattn_wo")):
        arrays[short] = np.ascontiguousarray(np.transpose(inputs[name], (1, 0)))
    lane, f32 = np.arange(P), np.float32
    arrays["identity"] = np.eye(P, dtype=f32)
    arrays["same_head"] = (lane[:, None] // DH == lane[None, :] // DH).astype(f32)
    arrays["head_of"] = (lane[:, None] // DH == np.arange(HG)[None, :]).astype(f32)
    arrays["earlier"] = (lane[:, None] < lane[None, :]).astype(f32)
    arrays["ones"] = np.ones((P, P), f32)
    arrays["zeros"] = np.zeros((P, D), f32)
    arrays["expert_no"] = np.tile(np.arange(E, dtype=f32), (P, 1))
    arrays["expert_base"] = np.tile(np.arange(E, dtype=f32) * CAP, (P, 1))
    arrays["token_no"] = (np.arange(B * NT)[None, :] * P + lane[:, None] + 1).astype(f32)
    arrays["dump_slot"] = (SLOTS + lane[:, None]).astype(f32)
    arrays["empty_row"] = (NTOK + 1 + lane[:, None]).astype(f32)
    arrays["table_init"] = np.zeros((SLOTS + P, 2), f32)

    nc = _bacc.Bacc("TRN2", target_bir_lowering=False, num_devices=1)
    t, ins = {}, {}
    for name, a in arrays.items():
        t[name] = nc.dram_tensor(f"in_{name}", a.shape, mybir.dt.from_np(a.dtype), kind="ExternalInput").ap()
        ins[f"in_{name}"] = a
    t["out"] = nc.dram_tensor("out_0", (B, T, D), F32, kind="ExternalOutput").ap()
    program(nc, t)
    r = _run(nc, [ins], core_ids=[0])
    return r.results[0]["out_0"]
```

```python
import numpy as np
from contextlib import ExitStack

import concourse.bass as bass
from concourse import mybir

F32 = mybir.dt.float32
F32R = mybir.dt.float32r
I32 = mybir.dt.int32
U32 = mybir.dt.uint32
ALU = mybir.AluOpType
ACT = mybir.ActivationFunctionType
AX = mybir.AxisListType

P = 128
B, T, M, D = 2, 1024, 2048, 512
H, DH = 16, 32
HG = P // DH
NG = H // HG
NC = D // P
NT = T // P
NTOK = B * T
MT = M // P
HALF = 512
NH = T // HALF
E, F, TOPK = 8, 1024, 2
NF = F // P
CAP = -(-5 * NTOK * TOPK // (4 * E))
NS = CAP // P
SLOTS = E * CAP
TABLES = 4
SCALE = float(DH) ** -0.5
EPS = 1e-5
STK = 3 * DH
SHIFT = 2
RSQRT_MAGIC = 0x5F3759DF


class Engine:

    def __init__(self, handle, sem):
        self.handle, self.sem, self.count, self.queue, self.seen = handle, sem, 0, [], {}

    def wait(self, *tokens):
        for token in tokens:
            if token is None:
                continue
            sem, value = token
            if self.seen.get(id(sem), 0) < value:
                self.seen[id(sem)] = value
                self.queue.append((None, (sem, value), {}, None, 0))

    def quiet(self, fn, *args, **kw):
        self.queue.append((fn, args, kw, None, 0))

    def run(self, fn, *args, **kw):
        self.count += 1
        self.queue.append((fn, args, kw, self.sem, 1))
        return (self.sem, self.count)

    def then(self, fn, *args, **kw):
        if self.count:
            self.wait((self.sem, self.count))
        return self.run(fn, *args, **kw)

    def dma(self, stream, out, in_, **kw):
        stream.count += 16
        self.queue.append((self.handle.dma_start, (out, in_), kw, stream.sem, 16))
        return (stream.sem, stream.count)

    def indirect(self, stream, **kw):
        stream.count += 16
        self.queue.append((self.handle.indirect_dma_start, (), kw, stream.sem, 16))
        return (stream.sem, stream.count)

    def last(self):
        return (self.sem, self.count) if self.count else None

    def emit(self):
        for fn, args, kw, sem, by in self.queue:
            if fn is None:
                self.handle.wait_ge(*args)
            elif sem is None:
                fn(*args, **kw)
            else:
                fn(*args, **kw).then_inc(sem, by)


class Stream:

    def __init__(self, sem):
        self.sem, self.count = sem, 0

    def all(self):
        return (self.sem, self.count) if self.count else None


def program(nc, t):
    ctx = ExitStack()
    with ctx:
        def sem(name):
            return ctx.enter_context(nc.semaphore(name))

        pe = Engine(nc.tensor, sem("pe_done"))
        dve = Engine(nc.vector, sem("dve_done"))
        act = Engine(nc.scalar, sem("act_done"))
        pool = Engine(nc.gpsimd, sem("pool_done"))
        sp = Engine(nc.sync, sem("sp_done"))
        engines = [pe, dve, act, pool, sp]
        streams = []

        def stream(name):
            streams.append(Stream(sem(name)))
            return streams[-1]

        def streams_of(name, n):
            return [stream(f"{name}{i}") for i in range(n)]

        def sb(scope, name, shape, dt=F32):
            return scope.enter_context(nc.sbuf_tensor(name, shape, dt))

        V, S, G = nc.vector, nc.scalar, nc.gpsimd

        q_parts = nc.dram_tensor("q_parts", (B, H, 2, DH, T), F32).ap()
        k_parts = nc.dram_tensor("k_parts", (B, H, 2, DH, M), F32).ap()
        v_rows = nc.dram_tensor("v_rows", (B, NG, P, MT, P), F32).ap()
        one_row_parts = nc.dram_tensor("one_row_parts", (SHIFT, M), F32).ap()
        x1_rows = nc.dram_tensor("x1_rows", (NTOK, D), F32).ap()
        x2_rows = nc.dram_tensor("x2_rows", (NTOK + P, D), F32).ap()
        y_rows = nc.dram_tensor("y_rows", (NTOK + P, D), F32).ap()
        slot_tables = [nc.dram_tensor(f"slot_table{i}", (SLOTS + P, 2), F32).ap() for i in range(TABLES)]

        pairs = [ctx.enter_context(nc.psum_tensor(f"banks{2 * i}", [P, 2, HALF], F32)) for i in range(4)]
        bank_free = [None] * 8

        def bank(i):
            return pairs[i // 2][:, i % 2, :]

        def accumulate(out, operands, start=True, stop=True):
            for n, (lhsT, rhs) in enumerate(operands):
                first, last = start and n == 0, stop and n == len(operands) - 1
                issue = pe.run if n == len(operands) - 1 else pe.quiet
                done = issue(nc.tensor.matmul, out, lhsT, rhs, start=first, stop=last)
            return done

        identity = sb(ctx, "identity", [P, P])
        same_head = sb(ctx, "same_head", [P, P])
        head_of = sb(ctx, "head_of", [P, HG])
        earlier = sb(ctx, "earlier", [P, P])
        ones = sb(ctx, "ones", [P, P])
        expert_no = sb(ctx, "expert_no", [P, E])
        expert_base = sb(ctx, "expert_base", [P, E])
        router_bias = sb(ctx, "router_bias", [P, E])
        router_w = sb(ctx, "router_w", [P, NC, E])
        token_no = sb(ctx, "token_no", [P, B * NT])
        empty_row = sb(ctx, "empty_row", [P, 1])
        dump_slot = sb(ctx, "dump_slot", [P, 1])
        stats = sb(ctx, "stats", [P, 6])
        mean_var = sb(ctx, "mean_var", [P, NT, 2])
        stats4 = sb(ctx, "stats4", [P, B * NT // 4, 6])
        neg_shift = sb(ctx, "neg_shift", [P, NT])
        rs_a, rs_b, rs_y = (sb(ctx, f"rsqrt_{n}", [P, NT]) for n in ("a", "b", "y"))
        const_in = stream("const_in")
        for tile, src in ((identity, t["identity"]), (same_head, t["same_head"]), (head_of, t["head_of"]),
                          (earlier, t["earlier"]), (ones, t["ones"]), (expert_no, t["expert_no"]),
                          (expert_base, t["expert_base"]), (token_no, t["token_no"]),
                          (dump_slot, t["dump_slot"]), (empty_row, t["empty_row"])):
            pool.dma(const_in, tile[:, :], src)
        pool.dma(const_in, router_bias[:, :], t["L0_ffn_router_b"].partition_broadcast(P))
        pool.dma(const_in, router_w[:, :, :], t["L0_ffn_router_w"].rearrange("(c p) e -> p c e", p=P))
        scratch_init = stream("scratch_init")
        for table in slot_tables:
            pool.dma(scratch_init, table, t["table_init"])
        pool.dma(scratch_init, x2_rows[NTOK:, :], t["zeros"])
        pool.dma(scratch_init, y_rows[NTOK:, :], t["zeros"])

        class Shelf:

            def __init__(self, at):
                self.at = at

            def __call__(self, name, shape, dt=F32):
                tensor = nc.alloc_sbuf_tensor_at(name, shape, dt, offset=self.at)
                size = 4 * int(np.prod(shape[1:]))
                self.at += -(-size // 32) * 32
                assert self.at <= nc.sbuf_top, name
                return tensor

        def rsqrt_of_variances(n, first=0):
            cols = slice(first, first + n)
            var, a, b, y = mean_var[:, cols, 1], rs_a[:, cols], rs_b[:, cols], rs_y[:, cols]
            dve.then(V.tensor_scalar, a, var, EPS, None, ALU.add)
            dve.then(V.tensor_scalar, y.bitcast(I32), a.bitcast(I32), 1, None, ALU.logical_shift_right)
            dve.then(V.tensor_scalar, y.bitcast(I32), y.bitcast(I32), -1.0, float(RSQRT_MAGIC), ALU.mult, ALU.add)
            dve.then(V.tensor_scalar, a, a, -0.5, None, ALU.mult)
            for _ in range(3):
                dve.then(V.tensor_tensor, b, y, y, ALU.mult)
                dve.then(V.tensor_tensor, b, b, a, ALU.mult)
                done = dve.then(V.scalar_tensor_tensor, y, b, 1.5, y, ALU.add, ALU.mult)
            return done

        def tile_statistics(row, n):
            dve.then(V.bn_stats, stats[:, :], row)
            return dve.then(V.bn_aggr, mean_var[:, n, :], stats[:, :])

        def normalise(out, row, n):
            return dve.run(V.tensor_scalar, out, row, mean_var[:, n, 0:1], rs_y[:, n:n + 1],
                           ALU.subtract, ALU.mult)

        def scale_and_shift(first, n):
            cols = slice(first, first + n)
            dve.wait(rsqrt_of_variances(n, first))
            return dve.run(V.scalar_tensor_tensor, neg_shift[:, cols], mean_var[:, cols, 0], -1.0,
                           rs_y[:, cols], ALU.mult, ALU.mult)

        def normalise_on_scalar(row, n):
            return act.run(S.activation, row, row, ACT.Identity, bias=neg_shift[:, n:n + 1], scale=rs_y[:, n:n + 1])

        def join(*extra):
            ends = [x.last() for x in engines] + [s.all() for s in streams] + list(extra)
            for engine in engines:
                engine.wait(*ends)

        HT = NT // NH
        b1c = sb(ctx, "b1c", [P, E, NF])
        table = sb(ctx, "table", [P, TABLES, E * NS, 2])
        tok = sb(ctx, "tok", [P, E * NS], U32)
        max4 = sb(ctx, "max4", [P, NT, HG, M // HALF])
        neg_max = sb(ctx, "neg_max", [P, NT, HG])
        max_hi = sb(ctx, "max_hi", [P, NT, HG], F32R)
        max_parts = sb(ctx, "max_parts", [P, NT, SHIFT, HG])
        TAIL_BYTES = 53760
        tail_base = (nc.sbuf_top - TAIL_BYTES) // 32 * 32
        loop_base = -(-nc.sbuf_base // 32) * 32

        put = Shelf(loop_base)
        NP = 4
        k_stack, q_stack = [put("k_stack0", [P, HG, M], F32R)], [put("q_stack0", [P, HG, T], F32R)]
        v_grp = [put(f"v_grp{i}", [P, MT, P]) for i in range(2)]
        probs = [put(f"probs{i}", [P, HG, HALF]) for i in range(NP)]
        shift_rows = put("shift_rows", [SHIFT * HG, T], F32R)
        context_base = put.at
        q_stack.append(put("q_stack1", [P, HG, T], F32R))
        k_stack.append(put("k_stack1", [P, HG, M], F32R))
        assert put.at <= tail_base
        put = Shelf(tail_base)
        heads_t = put("heads_t", [P, NG, T])
        xwo = put("xwo_t", [P, NC, D])
        xbo_row = put("xbo_row", [P, D])
        y_nat = [put(f"y_nat{i}", [P, HT, D]) for i in range(NH)]
        x2_t = [put(f"x2_t{i}", [P, NC, P]) for i in range(2)]
        num_c = put("num_c", [P, HALF])
        den_c = put("den_c", [P, HALF])
        lg, ex8, pr, ms, sv, kp = (put(f"rt_{n}", [P, HT, E]) for n in ("lg", "ex", "pr", "ms", "sv", "kp"))
        chosen, picked = (put(f"rt_{n}", [P, TOPK, HT, E]) for n in ("chosen", "picked"))
        slot = put("slot", [P, TOPK, HT])
        top8 = put("top8", [P, HT, 8])
        idx8 = put("idx8", [P, HT, 8], U32)
        idxf = put("idxf", [P, HT, 8])
        col = {n: put(f"col_{n}", [P, HT]) for n in ("max", "sum", "r", "s")}
        before = put("before", [P, HT + 1, E])
        slot_i = put("slot_i", [P, B * NT, TOPK], U32)
        entry = put("entry", [P, B * NT, TOPK, 2])

        put = Shelf(context_base)
        w_parts = {"k": [put(f"wk_{p}", [P, NC, D], F32R) for p in ("hi", "lo")],
                   "v": [put(f"wv_{p}", [P, NC, D], F32R) for p in ("hi", "lo")]}
        raw = [put(f"raw{i}", [P, NC, HALF]) for i in range(2)]
        src_parts = [[put(f"src{i}_{p}", [P, NC, HALF], F32R) for p in ("hi", "lo")] for i in range(2)]
        out_parts = [[put(f"out{i}_{p}", [P, HALF], F32R) for p in ("hi", "lo")] for i in range(2)]
        pre = [put(f"pre{i}", [P, HALF]) for i in range(2)]
        kv = put("kv", [P, NG, P + HG])
        kv_part = put("kv_part", [P, NG, P + 1])
        att_t = put("att_t", [P, NG, P])
        att = [put(f"att{i}", [P, D]) for i in range(2)]
        put = Shelf(loop_base)
        w_parts["q"] = [put(f"wq_{p}", [P, NC, D], F32R) for p in ("hi", "lo")]
        wo, wxq = put("wo", [P, NC, D]), put("wxq", [P, NC, D])
        k_half = put("k_half", [P, HT, D])
        v_half_at = put.at
        v_half = put("v_half", [P, HT, NG, P + 1])
        q_t_at = put.at
        q_t = put("q_t", [P, NG, T])
        x_nat = [put(f"x_nat{h}", [P, HT, D]) for h in range(NH)]
        x1_t = put("x1_t", [P, NC, HALF])
        low = [put(f"low{i}", [P, HALF]) for i in range(2)]
        bias_rows = {n: put(f"b{n}_row", [P, D]) for n in ("k", "v", "o")}
        bq_col = put("bq_col", [P, NG])
        den = put("den", [P, H])
        rden = put("rden", [P, H])
        assert put.at <= context_base
        put = Shelf(q_t_at)
        w_raw = {"v": put("wv_raw", [P, NC, D]), "q": put("wq_raw", [P, NC, D])}
        xw_raw = {"k": k_half, "v": Shelf(v_half_at)("xwv_raw", [P, NC, D])}

        def split(hi, lo, src, *ready):
            act.wait(*ready)
            rounded = act.run(S.activation, hi, src, ACT.Copy)
            dve.wait(rounded, *ready)
            return dve.run(V.tensor_tensor, lo, src, hi.bitcast(F32), ALU.subtract)

        def three_passes(left, right):
            return [(a, b_) for c in range(NC) for a, b_ in ((left[0][:, c], right[0][:, c]),
                                                             (left[0][:, c], right[1][:, c]),
                                                             (left[1][:, c], right[0][:, c]))]

        PASSES = 3

        def columns(parts, cols):
            return [part[:, :, cols] for part in parts]

        def transpose_tile(i, row):
            for c in range(NC):
                issue = pe.run if c == NC - 1 else pe.quiet
                done = issue(nc.tensor.transpose, bank(i)[:, c * P:(c + 1) * P], row[:, c * P:(c + 1) * P],
                             identity[:, :])
            return done

        class Ring:

            def __init__(self, *banks):
                self.banks, self.turn = banks, 0

            def __call__(self):
                i = self.banks[self.turn % len(self.banks)]
                self.turn += 1
                pe.wait(bank_free[i])
                return i

        def together(main, beside, beside_units, first, last):
            done = 0
            for i, _ in enumerate(main):
                while done < min(beside_units, beside_units * (i + 1 - first) // (last - first)):
                    next(beside, None)
                    done += 1
            for _ in beside:
                pass

        def snapshot():
            return [x.last() for x in engines] + [s.all() for s in streams]

        main_bank, side_bank = Ring(0, 1, 2, 3), Ring(4, 5, 6, 7)
        raw_in, part_out, v_out = streams_of("raw_in", 2), streams_of("part_out", 2), streams_of("v_out", 2)
        x_in, x1_out = streams_of("x_in", NH), streams_of("x1_out", NH)
        w_in = {n: stream(f"w{n}_in") for n in ("k", "v", "q", "o", "xq")}
        bias_in = stream("bias_in")
        MCH = M // HALF
        chunks = [t["x_t"][b][:, h * HALF:(h + 1) * HALF] for b in range(B) for h in range(NH)] + \
                 [t["ctx_t"][b][:, c * HALF:(c + 1) * HALF] for b in range(B) for c in range(MCH)]
        raw_ready, raw_free, chunk_ready, chunk_used = {}, [None, None], {}, {}

        def load_chunk(m):
            if m < len(chunks):
                sp.wait(raw_free[m % 2])
                raw_ready[m] = sp.dma(raw_in[m % 2], raw[m % 2][:, :, :], chunks[m].rearrange("(c p) n -> p c n", p=P))

        def split_chunk(m, c):
            if m < len(chunks):
                hi, lo = src_parts[m % 2]
                chunk_ready[m] = raw_free[m % 2] = split(hi[:, c, :], lo[:, c, :], raw[m % 2][:, c, :],
                                                         raw_ready[m], chunk_used.get(m - 2))

        w_raw["k"] = raw[1]
        w_loaded, w_ready, w_used = {}, {}, {}

        def load_weight(name, src, tile, *free):
            sp.wait(*free)
            w_loaded[name] = sp.dma(w_in[name], tile[:, :, :], t[src].rearrange("(c p) n -> p c n", p=P))

        def split_weight(name, source, c):
            hi, lo = w_parts[name]
            w_ready[name] = split(hi[:, c, :], lo[:, c, :], source[:, c, :], w_loaded[name], w_used.get(name))

        first_in, loaded = streams_of("first_in", 2 * NC), {}
        first_piece = {}
        for c in range(NC):
            rows = slice(c * P, (c + 1) * P)
            loaded["x", c] = sp.dma(first_in[2 * c], raw[0][:, c, :], chunks[0][rows, :])
            loaded["w", c] = sp.dma(first_in[2 * c + 1], w_raw["k"][:, c, :], t["wk_t"][rows, :])
        for n in ("k", "v", "o"):
            sp.dma(bias_in, bias_rows[n][:, :], t[f"L0_attn_b{n}"].partition_broadcast(P))
        bias_ready = sp.dma(bias_in, bq_col[:, :], t["bq_cols"])
        load_weight("v", "wv_t", w_raw["v"])
        load_weight("q", "wq_t", w_raw["q"])
        ones_out = stream("ones_out")
        tile_set = dve.run(V.memset, max_hi[:, :, :].bitcast(F32), 1.0)
        assert P * NT * HG == SHIFT * M
        ones_set = dve.run(V.memset, v_half[:, :, :, P:P + 1], 1.0)
        for c in range(NC):
            raw_ready[0], w_loaded["k"] = loaded["x", c], loaded["w", c]
            split_chunk(0, c)
            split_weight("k", w_raw["k"], c)
            first_piece[c] = w_ready["k"]
        raw_free[1] = w_ready["k"]
        for c in range(NC):
            split_weight("v", w_raw["v"], c)
        load_chunk(1)
        load_weight("o", "wo_t", wo)
        load_weight("xq", "xwq_t", wxq)
        dve.wait(bias_ready)
        act.wait(bias_ready)

        x_ready, x_used = {}, {}

        def fetch_x(b, h):
            if b < B:
                sp.wait(x1_out[h].all(), x_used.get(h))
                loaded = sp.dma(x_in[h], x_nat[h][:, :, :], t["x"][b][h * HALF:(h + 1) * HALF, :]
                                .rearrange("(n p) d -> p n d", p=P))
                pool.wait(loaded, bias_ready)
                for k in range(HT):
                    x_ready[b, h] = pool.run(G.tensor_tensor, x_nat[h][:, k, :], x_nat[h][:, k, :],
                                             bias_rows["o"][:, :], ALU.add)

        sp.wait(tile_set)
        sp.dma(ones_out, one_row_parts.rearrange("r (p n) -> (r p) n", n=NT * HG),
               max_hi[:, :, :].rearrange("p n j -> p (n j)").bitcast(F32))
        fetch_x(0, 0)
        fetch_x(0, 1)

        parts_turn = 0

        def store_parts(i, done, dest):
            nonlocal parts_turn
            s = parts_turn % 2
            parts_turn += 1
            hi, lo = out_parts[s]
            bank_free[i] = stored = split(hi[:, :], lo[:, :], bank(i), done, part_out[s].all())
            sp.wait(stored)
            for part, tile in enumerate((hi, lo)):
                sp.dma(part_out[s], dest[:, part], tile[:, :].bitcast(F32))

        low_free = [None, None]
        kv_used = [None]
        keys_used = [None]
        q_used = {}
        kv_ready, queries_ready = {}, {}

        def linear_attention_sums(b):
            for h in range(NH):
                m = b * NH + h
                src = src_parts[m % 2]
                load_chunk(m + 2)
                if m:
                    pe.wait(chunk_ready[m])
                for n in range(HT):
                    x_tile = columns(src, slice(n * P, (n + 1) * P))
                    i = main_bank()
                    terms = three_passes(x_tile, w_parts["k"])
                    for c in range(NC):
                        pe.wait(first_piece[c])
                        done = w_used["k"] = accumulate(bank(i), terms[c * PASSES:(c + 1) * PASSES],
                                                        start=c == 0, stop=c == NC - 1)
                    s = n % 2
                    dve.wait(done, low_free[s])
                    a = bank_free[i] = dve.run(V.tensor_tensor, pre[s][:, :], bank(i), bias_rows["k"][:, :], ALU.add)
                    below = dve.then(V.tensor_scalar, low[s][:, :], pre[s][:, :], 0.0, None, ALU.min)
                    act.wait(below)
                    exp_done = act.run(S.activation, low[s][:, :], low[s][:, :], ACT.Exp)
                    yield
                    pe.wait(w_ready["v"])
                    i = main_bank()
                    done = w_used["v"] = accumulate(bank(i), three_passes(x_tile, w_parts["v"]))
                    dve.wait(done, keys_used[0])
                    bank_free[i] = dve.run(V.tensor_tensor, v_half[:, n, :, 0:P],
                                           bank(i).rearrange("p (g e) -> p g e", g=NG),
                                           bias_rows["v"][:, :].rearrange("p (g e) -> p g e", g=NG), ALU.add)
                    dve.wait(exp_done)
                    keys_ready = low_free[s] = dve.run(V.scalar_tensor_tensor, k_half[:, n, :], pre[s][:, :], 0.0,
                                                       low[s][:, :], ALU.max, ALU.add)
                    if m == 0 and n == 1:
                        for c in range(NC):
                            split_weight("q", w_raw["q"], c)
                    split_chunk(m + 1, n)
                    yield
                for g in range(NG):
                    s = g % 2
                    pe.wait(w_ready["q"])
                    i = main_bank()
                    done = chunk_used[m] = accumulate(
                        bank(i), three_passes(columns(w_parts["q"], slice(g * P, (g + 1) * P)), src))
                    dve.wait(done, low_free[s])
                    below = dve.run(V.tensor_scalar, low[s][:, :], bank(i), bq_col[:, g:g + 1], 0.0, ALU.add, ALU.min)
                    act.wait(below)
                    act.run(S.activation, low[s][:, :], low[s][:, :], ACT.Exp)
                    above = bank_free[i] = act.run(S.activation, pre[s][:, :], bank(i), ACT.Relu,
                                                   bias=bq_col[:, g:g + 1])
                    dve.wait(above, q_used.get(h), w_ready["q"])
                    queries_ready[b, h] = low_free[s] = dve.run(V.tensor_tensor, q_t[:, g, h * HALF:(h + 1) * HALF],
                                                            pre[s][:, :], low[s][:, :], ALU.add)
                    yield
                    if g == 0:
                        pe.wait(keys_ready, ones_set)
                        for gg in range(NG):
                            i = main_bank()
                            done = keys_used[0] = accumulate(
                                bank(i)[:, 0:P + 1], [(k_half[:, n, gg * P:(gg + 1) * P], v_half[:, n, gg, :])
                                                      for n in range(HT)])
                            dve.wait(done)
                            if h == 0:
                                bank_free[i] = dve.run(V.tensor_copy, kv_part[:, gg, :], bank(i)[:, 0:P + 1])
                            else:
                                bank_free[i] = dve.run(V.tensor_tensor, kv_part[:, gg, :], bank(i)[:, 0:P + 1],
                                                       kv_part[:, gg, :], ALU.add)
                        if h == NH - 1:
                            dve.wait(bank_free[i], kv_used[0], const_in.all())
                            for gg in range(NG):
                                dve.run(V.tensor_tensor, kv[:, gg, 0:P], kv_part[:, gg, 0:P], same_head[:, :], ALU.mult)
                                kv_ready[b] = dve.run(V.tensor_scalar, kv[:, gg, P:P + HG], head_of[:, :],
                                                      kv_part[:, gg, P:P + 1], None, ALU.mult)
                        if m == B * NH - 1:
                            load_weight("k", "xwk_t", xw_raw["k"], keys_used[0])
                            load_weight("v", "xwv_t", xw_raw["v"], keys_used[0])
                        yield
                    elif m == B * NH - 1:
                        for c in range(NC):
                            if g < NG - 1:
                                name = ("k", "v")[g - 1]
                                split_weight(name, xw_raw[name], c)

        SUM_UNITS = NH * (2 * HT + NG + 1)

        def attention_rows(b):
            att_ready, att_used, att_t_ready, att_t_used = {}, {}, {}, [None]
            x1_ready, x1_t_ready = {}, {}

            def heads_of_tile(n):
                pe.wait(kv_ready[b], queries_ready[b, n // HT])
                dve.wait(att_used.get(n - 2))
                for pair in range(NG // 2):
                    i = side_bank()
                    for k in range(2):
                        g = 2 * pair + k
                        done = accumulate(bank(i)[:, k * (P + HG):(k + 1) * (P + HG)],
                                          [(q_t[:, g, n * P:(n + 1) * P], kv[:, g, :])])
                    both = bank(i)[:, 0:2 * (P + HG)].rearrange("p (k w) -> p k w", k=2)
                    hs = slice(pair * 2 * HG, (pair + 1) * 2 * HG)
                    dve.wait(done)
                    dve.run(V.tensor_scalar, den[:, hs].rearrange("p (k h) -> p k h", k=2),
                            both[:, :, P:P + HG], 1e-6, None, ALU.max)
                    dve.then(V.reciprocal, rden[:, hs], den[:, hs])
                    dve.wait(dve.last())
                    for k in range(2):
                        g = 2 * pair + k
                        bank_free[i] = att_ready[n] = dve.run(
                            V.tensor_tensor, att[n % 2][:, g * P:(g + 1) * P].rearrange("p (h e) -> p h e", h=HG),
                            both[:, k, 0:P].rearrange("p (h e) -> p h e", h=HG),
                            rden[:, g * HG:(g + 1) * HG].unsqueeze(2).to_broadcast([P, HG, DH]), ALU.mult)
                q_used[n // HT] = kv_used[0] = done

            def transpose_heads(n):
                pe.wait(att_ready[n], const_in.all())
                i = side_bank()
                done = att_used[n] = transpose_tile(i, att[n % 2])
                act.wait(done, att_t_used[0])
                att_t_ready[n] = bank_free[i] = act.run(
                    S.activation, att_t[:, :, :].rearrange("p g n -> p (g n)"), bank(i), ACT.Copy)

            def project(n):
                rows = x_nat[n // HT][:, n % HT, :]
                pe.wait(att_t_ready[n], w_loaded["o"])
                i = side_bank()
                done = att_t_used[0] = accumulate(bank(i), [(att_t[:, g, :], wo[:, g, :]) for g in range(NG)])
                dve.wait(done, x_ready[b, n // HT])
                bank_free[i] = dve.run(V.tensor_tensor, rows, bank(i), rows, ALU.add)
                tile_statistics(rows, n % HT)

            def stage(n):
                if 2 <= n:
                    project(n - 2)
                if 1 <= n <= NT:
                    transpose_heads(n - 1)
                if n < NT:
                    heads_of_tile(n)

            def layernorm(h):
                dve.wait(rsqrt_of_variances(HT))
                for k in range(HT):
                    x1_ready[h] = normalise(x_nat[h][:, k, :], x_nat[h][:, k, :], k)
                sp.wait(x1_ready[h])
                first = b * T + h * HALF
                sp.dma(x1_out[h], x1_rows[first:first + HALF, :].rearrange("(n p) d -> p n d", p=P), x_nat[h][:, :, :])

            def transpose_x1(h, first):
                for k in (first, first + 1):
                    pe.wait(x1_ready[h])
                    i = side_bank()
                    done = x_used[h] = transpose_tile(i, x_nat[h][:, k, :])
                    act.wait(done, x1_t_used[0])
                    x1_t_ready[h] = bank_free[i] = act.run(S.activation, x1_t[:, :, k * P:(k + 1) * P],
                                                           bank(i).rearrange("p (c n) -> p c n", c=NC), ACT.Copy)

            def queries(h, g):
                pe.wait(x1_t_ready[h], w_loaded["xq"])
                i = side_bank()
                done = x1_t_used[0] = accumulate(bank(i), [(wxq[:, c, g * P:(g + 1) * P], x1_t[:, c, :])
                                                           for c in range(NC)])
                store_parts(i, done, q_parts[b, g * HG:(g + 1) * HG, :, :, h * HALF:(h + 1) * HALF])

            for n in range(HT + 2):
                stage(n)
                yield
            layernorm(0)
            stage(HT + 2)
            yield
            transpose_x1(0, 0)
            stage(HT + 3)
            yield
            transpose_x1(0, 2)
            fetch_x(b + 1, 0)
            stage(HT + 4)
            yield
            queries(0, 0)
            stage(HT + 5)
            yield
            layernorm(1)
            for g in range(1, NG):
                queries(0, g)
                yield
            for k in (0, 2):
                transpose_x1(1, k)
                yield
            fetch_x(b + 1, 1)
            for g in range(NG):
                queries(1, g)
                yield

        x1_t_used = [None]
        ROW_UNITS = NT + 2 + NG - 1 + 2 + NG

        def context(b):
            for mc in range(MCH):
                m = B * NH + b * MCH + mc
                src = src_parts[m % 2]
                load_chunk(m + 2)
                pe.wait(chunk_ready[m], w_ready["k"], w_ready["v"])
                for u in range(NG):
                    i = main_bank()
                    terms = three_passes(columns(w_parts["k"], slice(u * P, (u + 1) * P)), src)
                    accumulate(bank(i), terms[:len(terms) // 2], stop=False)
                    yield
                    done = accumulate(bank(i), terms[len(terms) // 2:], start=False)
                    store_parts(i, done, k_parts[b, u * HG:(u + 1) * HG, :, :, mc * HALF:(mc + 1) * HALF])
                    yield
                    s = u % 2
                    i = main_bank()
                    terms = three_passes(columns(src, slice(u * P, (u + 1) * P)), w_parts["v"])
                    accumulate(bank(i), terms[:len(terms) // 2], stop=False)
                    yield
                    done = chunk_used[m] = accumulate(bank(i), terms[len(terms) // 2:], start=False)
                    act.wait(done, v_out[s].all(), low_free[s])
                    copied = bank_free[i] = act.run(S.activation, pre[s][:, :], bank(i), ACT.Copy)
                    sp.wait(copied)
                    sp.dma(v_out[s], v_rows[b, :, :, mc * HT + u, :].rearrange("g p e -> p g e"),
                           pre[s][:, :].rearrange("p (g e) -> p g e", g=NG))
                    split_chunk(m + 1, u)
                    yield

        CONTEXT_UNITS = MCH * 4 * NG
        assert HT == NC == NG == HALF // P

        for _ in linear_attention_sums(0):
            pass
        together(linear_attention_sums(1), attention_rows(0), ROW_UNITS, 0, SUM_UNITS)
        together(context(0), attention_rows(1), ROW_UNITS, 0, CONTEXT_UNITS - 2 * NG)
        attention_end = snapshot()

        x2_out, table_out = streams_of("x2_out", NH), streams_of("table_out", TABLES)
        groups = [(b, g) for b in range(B) for g in range(NG)]
        KCH = M // HALF
        k_in = [streams_of(f"k_in{i}_", KCH) for i in range(2)]
        q_in = [streams_of(f"q_in{i}_", NH) for i in range(2)]
        shift_in = streams_of("shift_in", 2)
        v_in = streams_of("v_in", 2)
        ones_in = stream("ones_in")
        xwo_in, y_in = stream("xwo_in"), streams_of("y_in", NH)
        k_ready, q_ready, v_ready, shift_ready = {}, {}, {}, {}

        def load_k(n, c, free=None):
            if n >= len(groups) or c >= KCH:
                return
            b, g = groups[n]
            src = k_parts[b, g * HG:(g + 1) * HG, :, :, c * HALF:(c + 1) * HALF]
            dst = k_stack[n % 2][:, :, c * HALF:(c + 1) * HALF].bitcast(F32)
            sp.wait(free)
            sp.dma(k_in[n % 2][c], dst[0:2 * DH], src.rearrange("j l r m -> (l r) j m"))
            k_ready[n, c] = sp.dma(k_in[n % 2][c], dst[2 * DH:STK], src[:, 0].rearrange("j r m -> r j m"))

        def load_q(n, h, free=None):
            if n >= len(groups):
                return
            b, g = groups[n]
            src = q_parts[b, g * HG:(g + 1) * HG, :, :, h * HALF:(h + 1) * HALF]
            dst = q_stack[n % 2][:, :, h * HALF:(h + 1) * HALF].bitcast(F32)
            sp.wait(free)
            sp.dma(q_in[n % 2][h], dst[0:DH], src[:, 0].rearrange("j r m -> r j m"))
            q_ready[n, h] = sp.dma(q_in[n % 2][h], dst[DH:STK], src.rearrange("j l r m -> (l r) j m"))

        def load_v(n, free=None):
            if n >= len(groups):
                return
            b, g = groups[n]
            sp.wait(free)
            v_ready[n] = sp.dma(v_in[n % 2], v_grp[n % 2][:, :, :], v_rows[b, g])

        NUM, DEN = 6, 7
        next_score_bank, next_s_bank = Ring(0, 1, 2), Ring(3, 4, 5)

        def max_pass(n, ring):
            ks, qs = k_stack[n % 2], q_stack[n % 2]
            for mc in range(KCH):
                pe.wait(k_ready[n, mc])
                for nt in range(NT):
                    pe.wait(q_ready[n, nt * P // HALF])
                    for j in range(HG):
                        i = ring()
                        done = accumulate(bank(i), [(qs[0:STK, j, nt * P:(nt + 1) * P],
                                                     ks[0:STK, j, mc * HALF:(mc + 1) * HALF])])
                        dve.wait(done)
                        bank_free[i] = dve.run(V.reduce_max, max4[:, nt, j, mc:mc + 1], bank(i), AX.X)
                        yield

        shift_taken = [None]
        SHIFT_UNITS = 4
        PREPARE_UNITS = KCH * NT * HG + SHIFT_UNITS

        def prepare(n, ring):
            yield from max_pass(n, ring)
            dve.wait(shift_taken[0])
            dve.then(V.tensor_reduce, neg_max[:, :, :], max4[:, :, :, :], AX.X, ALU.max)
            dve.then(V.tensor_scalar, neg_max[:, :, :], neg_max[:, :, :], -1.0, None, ALU.mult)
            dve.then(V.tensor_copy, max_hi[:, :, :], neg_max[:, :, :])
            dve.then(V.tensor_copy, max_parts[:, :, 0, :], max_hi[:, :, :].bitcast(F32))
            parts_ready = dve.then(V.tensor_tensor, max_parts[:, :, 1, :], neg_max[:, :, :],
                                   max_hi[:, :, :].bitcast(F32), ALU.subtract)
            for _ in range(SHIFT_UNITS):
                yield
            pe.wait(parts_ready)
            for h in range(NH):
                i = ring()
                for q in range(HALF // P):
                    nt = h * (HALF // P) + q
                    done = accumulate(bank(i)[0:SHIFT * HG, q * P:(q + 1) * P],
                                      [(max_parts[:, nt, :, :].rearrange("p l j -> p (l j)"), identity[:, :])])
                act.wait(done, shift_in[(n - 1) % 2].all())
                rows = bank_free[i] = act.run(S.activation, shift_rows[:, h * HALF:(h + 1) * HALF],
                                              bank(i)[0:SHIFT * HG, :], ACT.Copy)
            shift_taken[0] = done
            sp.wait(rows, q_free[n % 2])
            for part in range(SHIFT):
                shift_ready[n] = sp.dma(shift_in[n % 2], q_stack[n % 2][STK + part:STK + part + 1, :, :].bitcast(F32),
                                        shift_rows[part * HG:(part + 1) * HG, :].bitcast(F32))

        q_free = [None, None]
        probs_free = [None] * NP
        probs_turn = 0
        heads_free, heads_ready, rows_used = {}, {}, {}

        ones_ready = {}

        def one_rows(n):
            for j in range(HG):
                ones_ready[n] = sp.dma(ones_in, k_stack[n][STK:STK + SHIFT, j, :].bitcast(F32), one_row_parts)

        def first_group():
            for i, _ in enumerate(prepare(0, side_bank)):
                if i % (NT * HG) == NT:
                    load_k(0, 1 + i // (NT * HG))
                yield
            load_v(0)

        sp.wait(*attention_end)
        load_q(0, 0)
        load_k(0, 0)
        load_q(0, 1)
        one_rows(0)
        together(context(1), first_group(), PREPARE_UNITS + 1, 3 * NG, CONTEXT_UNITS - 2)
        for engine in (dve, act, pool):
            engine.wait(*attention_end)
        context_end = snapshot()

        rows_ready = {}

        def fetch_rows(b, hh):
            assert b == 0 or (b - 1, hh) in rows_used
            ys = y_nat[hh]
            sp.wait(x2_out[hh].all(), rows_used.get((b - 1, hh)))
            y_ready = sp.dma(y_in[hh], ys[:, :, :], x1_rows[(b * NT + hh * HT) * P:(b * NT + (hh + 1) * HT) * P, :]
                             .rearrange("(n p) d -> p n d", p=P))
            yield
            pool.wait(y_ready, xwo_ready)
            for k in range(HT):
                rows_ready[b, hh, k] = pool.run(G.tensor_tensor, ys[:, k, :], ys[:, k, :], xbo_row[:, :], ALU.add)
                yield

        statistics_used = [None]

        def project_rows(b, hh, chunks):
            ys = y_nat[hh]
            for k in range(HT):
                n = hh * HT + k
                pe.wait(*(heads_ready[hh, g, k] for g in chunks), xwo_ready)
                i = next_s_bank()
                done = accumulate(bank(i), [(heads_t[:, g, n * P:(n + 1) * P], xwo[:, g, :]) for g in chunks])
                for g in chunks:
                    heads_free[hh, g] = done
                dve.wait(done, rows_ready[b, hh, k])
                bank_free[i] = dve.run(V.tensor_tensor, ys[:, k, :], bank(i), ys[:, k, :], ALU.add)
                if NG - 1 in chunks:
                    tile_statistics(ys[:, k, :], k)
                yield

        def rows_of(b, hh):
            ys = y_nat[hh]
            dve.wait(statistics_used[0])
            yield from project_rows(b, hh, [NG - 1])
            act.wait(scale_and_shift(0, HT))
            x2_ready = []
            x2_t_ready, x2_t_free = [None] * HT, [None] * HT

            def transpose_rows(k):
                pe.wait(x2_ready[k])
                i = next_s_bank()
                for c in range(NC):
                    issue = pe.run if c == NC - 1 else pe.quiet
                    done = issue(nc.tensor.transpose, bank(i)[:, c * P:(c + 1) * P],
                                 ys[:, k, c * P:(c + 1) * P], identity[:, :])
                rows_used[b, hh] = done
                act.wait(done, x2_t_free[k - 2] if k >= 2 else None)
                x2_t_ready[k] = bank_free[i] = act.run(
                    S.activation, x2_t[k % 2][:, :, :].rearrange("p c n -> p (c n)"), bank(i), ACT.Copy)

            def logits(k):
                pe.wait(x2_t_ready[k])
                i = next_s_bank()
                x2_t_free[k] = done = accumulate(bank(i)[:, 0:E], [(x2_t[k % 2][:, c, :], router_w[:, c, :])
                                                                  for c in range(NC)])
                dve.wait(done)
                bank_free[i] = dve.run(V.tensor_tensor, lg[:, k, :], bank(i)[:, 0:E], router_bias[:, :], ALU.add)

            for k in range(HT + 2):
                if k < HT:
                    x2_ready.append(normalise_on_scalar(ys[:, k, :], k))
                if k == HT - 1:
                    statistics_used[0] = x2_ready[-1]
                    sp.wait(x2_ready[-1])
                    first = (b * NT + hh * HT) * P
                    for rows in (x2_rows, y_rows):
                        sp.dma(x2_out[hh], rows[first:first + HT * P, :].rearrange("(n p) d -> p n d", p=P),
                               ys[:, :, :])
                if k >= 3:
                    logits(k - 3)
                if k >= 2:
                    transpose_rows(k - 2)
                yield
            logits(HT - 1)
            yield

            def per_tile(x):
                return x[:, :].unsqueeze(2).to_broadcast([P, HT, E])

            def per_expert(x):
                return x[:, :].unsqueeze(1).to_broadcast([P, HT, E])

            dve.then(V.reduce_max, col["max"][:, :], lg[:, :, :], AX.X)
            lg_ready = dve.then(V.tensor_tensor, lg[:, :, :], lg[:, :, :], per_tile(col["max"]), ALU.subtract)
            act.wait(lg_ready)
            ex_ready = act.run(S.activation, ex8[:, :, :], lg[:, :, :], ACT.Exp)
            yield
            dve.wait(ex_ready)
            dve.then(V.reduce_sum, col["sum"][:, :], ex8[:, :, :], AX.X)
            dve.then(V.reciprocal, col["r"][:, :], col["sum"][:, :])
            dve.wait(dve.then(V.tensor_tensor, pr[:, :, :], ex8[:, :, :], per_tile(col["r"]), ALU.mult))
            yield
            for k in range(HT):
                top_done = dve.run(V.max, top8[:, k, :], pr[:, k, :])
            dve.wait(top_done)
            for k in range(HT):
                dve.run(V.max_index, idx8[:, k, :], top8[:, k, :], pr[:, k, :])
            dve.then(V.tensor_copy, idxf[:, :, :], idx8[:, :, :])
            yield
            dve.then(V.tensor_tensor, chosen[:, :, :, :],
                     expert_no[:, :].unsqueeze(1).unsqueeze(1).to_broadcast([P, TOPK, HT, E]),
                     idxf[:, :, 0:TOPK].rearrange("p n k -> p k n").unsqueeze(3).to_broadcast([P, TOPK, HT, E]),
                     ALU.is_equal)
            dve.then(V.tensor_tensor, ms[:, :, :], chosen[:, 0], chosen[:, 1], ALU.add)
            dve.then(V.tensor_copy, before[:, 0, :], before[:, HT, :])
            for k in range(HT):
                before_ready = dve.then(V.tensor_tensor, before[:, k + 1, :], before[:, k, :], ms[:, k, :],
                                        ALU.add)
            yield
            pe.wait(before_ready)
            i = next_s_bank()
            for k in range(HT):
                ranks_done = accumulate(bank(i)[:, k * E:(k + 1) * E],
                                        [(earlier[:, :], ms[:, k, :]), (ones[:, :], before[:, k, :])])
            rank = bank(i)[:, 0:HT * E].rearrange("p (n e) -> p n e", n=HT)
            dve.then(V.tensor_tensor, col["s"][:, :], top8[:, :, 0], top8[:, :, 1], ALU.add)
            dve.then(V.tensor_scalar, col["s"][:, :], col["s"][:, :], 1e-9, None, ALU.max)
            dve.then(V.reciprocal, col["r"][:, :], col["s"][:, :])
            dve.wait(ranks_done)
            dve.run(V.tensor_scalar, kp[:, :, :], rank, float(CAP), None, ALU.is_lt)
            bank_free[i] = dve.run(V.tensor_tensor, sv[:, :, :], rank, per_expert(expert_base), ALU.add)
            yield
            dve.then(V.scalar_tensor_tensor, sv[:, :, :], sv[:, :, :], dump_slot[:, :], kp[:, :, :],
                     ALU.subtract, ALU.mult)
            dve.then(V.tensor_tensor, picked[:, :, :, :], chosen[:, :, :, :],
                     sv[:, :, :].unsqueeze(1).to_broadcast([P, TOPK, HT, E]), ALU.mult)
            dve.then(V.reduce_sum, slot[:, :, :], picked[:, :, :, :], AX.X)
            dve.then(V.tensor_scalar, slot[:, :, :], slot[:, :, :], dump_slot[:, :], None, ALU.add)
            tiles = slice(b * NT + hh * HT, b * NT + (hh + 1) * HT)
            dve.then(V.tensor_copy, slot_i[:, tiles, :].rearrange("p n k -> p k n"), slot[:, :, :])
            for k in range(TOPK):
                dve.run(V.tensor_tensor, entry[:, tiles, k, 1], top8[:, :, k], col["r"][:, :], ALU.mult)
                entry_ready = dve.run(V.tensor_copy, entry[:, tiles, k, 0], token_no[:, tiles])
            yield
            pool.wait(entry_ready, scratch_init.all())
            for n in range(tiles.start, tiles.stop):
                for k in range(TOPK):
                    which = (n % 2) * TOPK + k
                    pool.wait(table_out[which].all())
                    pool.indirect(table_out[which], out=slot_tables[which],
                                  out_offset=bass.IndirectOffsetOnAxis(ap=slot_i[:, n, k:k + 1], axis=0),
                                  in_=entry[:, n, k, :], in_offset=None)
                yield

        sides = []

        def side():
            while sides:
                try:
                    next(sides[0])
                    return
                except StopIteration:
                    sides.pop(0)

        divisions = []
        PIECE = HALF // 8

        def divide(pieces):
            nonlocal divided
            for _ in range(min(pieces, len(divisions))):
                copied, b, g, h, q = divisions.pop(0)
                dve.wait(copied, heads_free.get((h, g)))
                cols = slice(q * PIECE, (q + 1) * PIECE)
                dve.run(V.reciprocal, den_c[:, cols], den_c[:, cols])
                divided = heads_ready[h, g, q * PIECE // P] = dve.then(
                    V.tensor_tensor, heads_t[:, g, h * HALF + q * PIECE:h * HALF + (q + 1) * PIECE],
                    num_c[:, cols], den_c[:, cols], ALU.mult)
                if q == HALF // PIECE - 1:
                    if g == NG - 2:
                        sides.append(project_rows(b, h, list(range(NG - 1))))
                    if g == NG - 1:
                        sides.append(rows_of(b, h))

        pending = []
        clock = 0

        def denominators(until):
            while pending and pending[0][0] <= until:
                _, tiles, summed, mt, b, g, h = pending.pop(0)
                pe.wait(summed)
                if mt == 1:
                    pe.wait(bank_free[DEN])
                for q in tiles:
                    for j in range(HG):
                        den_done = accumulate(bank(DEN)[j * DH:(j + 1) * DH, :],
                                              [(ones[:, 0:DH], probs[q][:, j, :])],
                                              start=mt == 1, stop=mt == MT - 1 and q == tiles[-1])
                    probs_free[q] = (den_done,)
                if mt == MT - 1:
                    act.wait(den_done, divided)
                    bank_free[DEN] = copied = act.run(S.activation, den_c[:, :], bank(DEN), ACT.Copy)
                    divisions.extend((copied, b, g, h, q) for q in range(HALF // PIECE))

        divided = None
        for n, (b, g) in enumerate(groups):
            ks, qs, vs = k_stack[n % 2], q_stack[n % 2], v_grp[n % 2]
            ahead = prepare(n + 1, next_s_bank) if n + 1 < len(groups) else None
            todo = PREPARE_UNITS if ahead else 0
            steps = [(h, mt) for h in range(NH) for mt in range(MT)]
            FIRST, LAST = (0 if n else 4), 30
            issued = 0
            allowed = 0

            def maxima(count=1):
                nonlocal issued, ahead
                while ahead and count and issued < allowed:
                    next(ahead)
                    issued += 1
                    count -= 1
                if ahead and issued == todo:
                    for _ in ahead:
                        pass
                    ahead = None

            def scores(h, mt, p, heads):
                pe.wait(k_ready[n, mt * P // HALF], q_ready[n, h], shift_ready[n], ones_ready.get(n))
                act.wait(*(probs_free[p] or ()))
                for j in heads:
                    i = next_score_bank()
                    done = accumulate(bank(i), [(ks[0:STK + SHIFT, j, mt * P:(mt + 1) * P],
                                                 qs[0:STK + SHIFT, j, h * HALF:(h + 1) * HALF])])
                    act.wait(done)
                    exp_done = bank_free[i] = act.run(S.activation, probs[p][:, j, :], bank(i), ACT.Exp,
                                                      scale=SCALE)
                maxima()
                return p, exp_done, done

            def next_probs():
                nonlocal probs_turn
                probs_turn += 1
                return (probs_turn - 1) % NP

            current = scores(*steps[0], next_probs(), range(HG))
            for s, (h, mt) in enumerate(steps):
                p, exp_done, _ = current
                denominators(clock)
                maxima()
                if ahead:
                    allowed = max(0, min(todo, -(-todo * (s + 1 - FIRST) // (LAST - FIRST))))
                if n == 0 and s == 1:
                    for engine in (sp, act, dve, pool):
                        engine.wait(*context_end)
                    for half in range(NH):
                        load_q(1, half)
                    for c in range(KCH):
                        load_k(1, c)
                    one_rows(1)
                    load_v(1)
                    sp.dma(xwo_in, xwo[:, :, :], t["xwo_t"].rearrange("(c p) n -> p c n", p=P))
                    xwo_ready = sp.dma(xwo_in, xbo_row[:, :], t["L0_xattn_bo"].partition_broadcast(P))
                    dve.run(V.memset, before[:, :, :], 0.0)
                if s + 1 < len(steps):
                    p_next = next_probs()
                    scores(*steps[s + 1], p_next, range(HG // 2))
                pe.wait(exp_done, v_ready[n])
                if mt == 0:
                    pe.wait(bank_free[NUM])
                for j in range(HG):
                    num_done = accumulate(bank(NUM)[j * DH:(j + 1) * DH, :],
                                          [(vs[:, mt, j * DH:(j + 1) * DH], probs[p][:, j, :])],
                                          start=mt == 0, stop=mt == MT - 1)
                if mt == MT - 1:
                    divide(len(divisions))
                    act.wait(num_done, divided)
                    bank_free[NUM] = act.run(S.activation, num_c[:, :], bank(NUM), ACT.Copy)
                maxima()
                if s + 1 < len(steps):
                    following = scores(*steps[s + 1], p_next, range(HG // 2, HG))
                    h2, mt2 = steps[s + 1]
                    if h2 == NH - 1 and mt2 % (HALF // P) == HALF // P - 1:
                        load_k(n + 2, mt2 * P // HALF, following[2])
                if s == MT - 1:
                    load_q(n + 2, 0, following[2])
                if mt % 2 == 0:
                    even = p, num_done
                elif n == len(groups) - 1 and s == len(steps) - 1:
                    pending.append((clock + 2, (even[0], p), exp_done, mt, b, g, h))
                else:
                    adder, handle = (dve, V) if n == len(groups) - 1 else (pool, G)
                    adder.wait(exp_done, even[1])
                    summed = adder.run(handle.tensor_tensor, probs[even[0]][:, :, :], probs[even[0]][:, :, :],
                                       probs[p][:, :, :], ALU.add)
                    probs_free[p] = (num_done, summed)
                    pending.append((clock + 2, (even[0],), summed, mt, b, g, h))
                maxima(2)
                divide(1 if n < len(groups) - 1 else 4)
                if n == len(groups) - 1:
                    side()
                    side()
                    side()
                elif s % 2:
                    side()
                if g == NG - 2 and mt == 2:
                    sides.append(fetch_rows(b, h))
                clock += 1
                current = following
            q_free[n % 2] = current[2]
            load_q(n + 2, 1, current[2])
            load_v(n + 2, num_done)
            if n == len(groups) - 1:
                denominators(clock + 3)
                loop_end = [x.last() for x in engines]
                divide(len(divisions))

        y_add, out_done = stream("y_add"), streams_of("out_done", 2)
        put = Shelf(loop_base)
        w1_raw = put("w1_raw", [P, NC, F])
        w2_raw = put("w2_raw", [P, NF, D])
        w1_hi, w1_lo = (put(f"w1_{n}", [P, NC, F], F32R) for n in ("hi", "lo"))
        w2_hi, w2_lo = (put(f"w2_{n}", [P, NF, D], F32R) for n in ("hi", "lo"))
        xe_hi, xe_lo = (put(f"xe_{n}", [P, NC, CAP], F32R) for n in ("hi", "lo"))
        hid_hi = put("hid_hi", [P, NF, CAP], F32R)
        xg = [put(f"xg{i}", [P, D]) for i in range(NS)]
        assert put.at <= tail_base
        put = Shelf(tail_base)
        hid_lo = put("hid_lo", [P, NF, CAP], F32R)
        hid = [put(f"hid{i}", [P, CAP]) for i in range(2)]
        eo = [put(f"eo{i}", [P, D]) for i in range(3)]
        b2s = [put(f"b2s{i}", [P, D]) for i in range(2)]
        w1_in, w2_in, b2_in = stream("w1_in"), stream("w2_in"), streams_of("b2_in", 2)
        b1_in, table_in = stream("b1_in"), streams_of("table_in", TABLES)
        xg_in = streams_of("xg_in", NS)

        raw_ready, split_ready, raw_free = {}, {}, {}

        def fetch_w1(e):
            if e < E:
                sp.wait(raw_free.get(1))
                raw_ready[e, 1] = sp.dma(w1_in, w1_raw[:, :, :],
                                         t["L0_ffn_w1"][e].rearrange("(c p) f -> p c f", p=P))

        def fetch_w2(e):
            if e < E:
                sp.wait(raw_free.get(2))
                raw_ready[e, 2] = sp.dma(w2_in, w2_raw[:, :, :],
                                         t["L0_ffn_w2"][e].rearrange("(c p) d -> p c d", p=P))

        def split_w1(e, c, used):
            if e < E:
                dve.wait(used)
                split_ready[e, 1] = raw_free[1] = split(w1_hi[:, c, :], w1_lo[:, c, :], w1_raw[:, c, :],
                                                        used, raw_ready[e, 1])

        def split_w2(e, f, used):
            if e < E:
                dve.wait(used)
                split_ready[e, 2] = raw_free[2] = split(w2_hi[:, f:f + 2, :], w2_lo[:, f:f + 2, :],
                                                        w2_raw[:, f:f + 2, :], used, raw_ready[e, 2])

        sp.wait(*loop_end)
        fetch_w1(0)
        fetch_w2(0)
        b1_ready = sp.dma(b1_in, b1c[:, :, :], t["b1_cols"])
        while sides:
            side()
        tail_end = [x.last() for x in engines] + [s.all() for s in x2_out]
        act.wait(*loop_end)
        dve.wait(*loop_end)
        pool.wait(*loop_end)
        for c in range(NC):
            split_w1(0, c, None)
        for f in range(0, NF, 2):
            split_w2(0, f, None)
        sp.wait(*(x.all() for x in table_out))
        for i in range(TABLES):
            sp.dma(table_in[i], table[:, i, :, :].rearrange("p (e i) w -> p e i w", e=E),
                   slot_tables[i][0:SLOTS, :].rearrange("(e p i) w -> p e i w", p=P, i=NS))
        dve.wait(*(x.all() for x in table_in))
        dve.run(V.tensor_tensor, table[:, 0], table[:, 0], table[:, 1], ALU.add)
        dve.run(V.tensor_tensor, table[:, 2], table[:, 2], table[:, 3], ALU.add)
        dve.then(V.tensor_tensor, table[:, 0], table[:, 0], table[:, 2], ALU.add)
        number, weight = table[:, 0, :, 0], table[:, 0, :, 1]
        spare = table[:, 1, :, 0]
        dve.then(V.tensor_scalar, spare, number, 0.0, empty_row[:, :], ALU.is_equal, ALU.mult)
        dve.then(V.tensor_tensor, spare, spare, number, ALU.add)
        dve.then(V.tensor_scalar, spare, spare, -1.0, None, ALU.add)
        tok_ready = dve.then(V.tensor_copy, tok[:, :], spare)
        pool.wait(tok_ready, *(x.all() for x in x2_out))
        act.wait(b1_ready)
        xg_ready, xg_free = {}, [None] * NS

        def gather(e, i):
            if e < E:
                pool.wait(xg_free[i])
                xg_ready[e, i] = pool.indirect(
                    xg_in[i], out=xg[i][:, :], out_offset=None, in_=x2_rows,
                    in_offset=bass.IndirectOffsetOnAxis(ap=tok[:, e * NS + i:e * NS + i + 1], axis=0))

        next_t_bank, next_o_bank = Ring(4, 5), Ring(6, 7)
        xe_ready = {}

        def transposes(e, i, used):
            if e >= E:
                return
            pe.wait(xg_ready[e, i])
            k = next_t_bank()
            for c in range(NC):
                issue = pe.run if c == NC - 1 else pe.quiet
                done = issue(nc.tensor.transpose, bank(k)[:, c * P:(c + 1) * P], xg[i][:, c * P:(c + 1) * P],
                             identity[:, :])
            xg_free[i] = done
            dve.wait(used)
            cols = slice(i * P, (i + 1) * P)
            xe_ready[e] = bank_free[k] = split(xe_hi[:, :, cols], xe_lo[:, :, cols],
                                               bank(k).rearrange("p (c n) -> p c n", c=NC), done, used)

        for i in range(NS):
            gather(0, i)
        for i in range(NS):
            transposes(0, i, None)
            gather(1, i)
        sp.wait(xg_ready[0, NS - 1])
        fetch_w1(1)
        for engine in (pool, act, dve, sp):
            engine.wait(*tail_end)
        eo_turn = 0
        eo_free, hid_free = [None] * 3, [None] * 2
        b2_ready, b2_free = {}, [None] * 2
        out_done_e, hid_ready = None, {}
        HC = CAP // 2
        PARTS1 = ((w1_hi, xe_hi), (w1_hi, xe_lo), (w1_lo, xe_hi))
        PARTS2 = ((hid_hi, w2_hi), (hid_hi, w2_lo), (hid_lo, w2_hi))
        for e in range(E):
            sp.wait(b2_free[e % 2])
            b2_ready[e] = sp.dma(b2_in[e % 2], b2s[e % 2][:, :], t["L0_ffn_b2"][e].partition_broadcast(P))
            pe.wait(split_ready[e, 1], xe_ready[e])
            for f in range(NF):
                pair = f % 2
                pe.wait(bank_free[2 * pair])
                terms = [(w[:, c, f * P:(f + 1) * P], x[:, c]) for c in range(NC) for w, x in PARTS1]
                for n, (w, x) in enumerate(terms):
                    for h in range(2):
                        last = n == len(terms) - 1
                        issue = pe.run if last and h else pe.quiet
                        done = issue(nc.tensor.matmul, pairs[pair][:, h, 0:HC], w, x[:, h * HC:(h + 1) * HC],
                                     start=n == 0, stop=last)
                act.wait(done, hid_free[f % 2])
                hid_done = bank_free[2 * pair] = bank_free[2 * pair + 1] = act.run(
                    S.activation, hid[f % 2][:, :].rearrange("p (h n) -> p h n", h=2), pairs[pair][:, :, 0:HC],
                    ACT.Gelu, bias=b1c[:, e, f:f + 1])
                dve.wait(out_done_e)
                hid_ready[f] = hid_free[f % 2] = split(hid_hi[:, f, :], hid_lo[:, f, :], hid[f % 2][:, :],
                                                       hid_done, out_done_e)
                if e and f < NF // 2:
                    split_w2(e, 2 * f, out_done_e)
            fetch_w2(e + 1)
            hidden_done = done
            pe.wait(split_ready[e, 2])
            for i in range(NS):
                transposes(e + 1, i, hidden_done)
                gather(e + 2, i)
                k = next_o_bank()
                for f in range(NF):
                    pe.wait(hid_ready[f])
                    out_done_e = done = accumulate(bank(k), [(a[:, f, i * P:(i + 1) * P], w[:, f, :])
                                                             for a, w in PARTS2], start=f == 0, stop=f == NF - 1)
                s = eo_turn % 3
                eo_turn += 1
                dve.wait(done, b2_ready[e], eo_free[s])
                b2_free[e % 2] = bank_free[k] = dve.run(V.tensor_tensor, eo[s][:, :], bank(k), b2s[e % 2][:, :],
                                                        ALU.add)
                eo_ready = dve.then(V.tensor_scalar, eo[s][:, :], eo[s][:, :],
                                    weight[:, e * NS + i:e * NS + i + 1], None, ALU.mult)
                pool.wait(eo_ready, y_add.all())
                eo_free[s] = pool.indirect(
                    y_add, out=y_rows, in_=eo[s][:, :], in_offset=None, compute_op=ALU.add,
                    out_offset=bass.IndirectOffsetOnAxis(ap=tok[:, e * NS + i:e * NS + i + 1], axis=0))
                if i < NC:
                    split_w1(e + 1, i, hidden_done)
            fetch_w1(e + 2)
        added = y_add.all()
        join()

        with ExitStack() as scope:
            yf = Shelf(loop_base)("y_final", [P, B * NT, D])
            normalised = {}
            y_final_in = streams_of("yf_in", 4)
            Q4 = B * NT // 4
            for q in range(4):
                rows = y_rows[q * Q4 * P:(q + 1) * Q4 * P, :].rearrange("(n p) d -> p n d", p=P)
                sp.wait(added)
                sp.dma(y_final_in[q], yf[:, q * Q4:(q + 1) * Q4, :], rows)
            out_flat = t["out"].rearrange("b s d -> (b s) d")
            for q in range(4):
                dve.wait(y_final_in[q].all())
                first = q % 2 * Q4
                dve.wait(normalised.get(q - 2))
                for n in range(Q4):
                    done = dve.run(V.bn_stats, stats4[:, n, :], yf[:, q * Q4 + n, :])
                dve.wait(done)
                for n in range(Q4):
                    dve.run(V.bn_aggr, mean_var[:, first + n, :], stats4[:, n, :])
                act.wait(scale_and_shift(first, Q4))
                for n in range(Q4):
                    normalised[q] = done = normalise_on_scalar(yf[:, q * Q4 + n, :], first + n)
                act.wait(done)
                act.dma(out_done[q % 2], out_flat[q * Q4 * P:(q + 1) * Q4 * P, :].rearrange("(n p) d -> p n d", p=P),
                        yf[:, q * Q4:(q + 1) * Q4, :])
            act.wait(*[s.all() for s in streams])

        block = ctx.enter_context(nc.Block())

        @block.tensor
        def _(_eng):
            pe.emit()

        @block.vector
        def _(_eng):
            dve.emit()

        @block.scalar
        def _(_eng):
            act.emit()

        @block.gpsimd
        def _(_eng):
            pool.emit()

        @block.sync
        def _(_eng):
            sp.emit()


def kernel(**inputs):
    import concourse.bacc as _bacc
    from concourse.bass_utils import run_bass_kernel_spmd as _run

    arrays = {n: np.ascontiguousarray(inputs[n]) for n in (
        "x", "L0_attn_bk", "L0_attn_bv", "L0_attn_bo", "L0_xattn_bo", "L0_ffn_router_w",
        "L0_ffn_router_b", "L0_ffn_w1", "L0_ffn_w2", "L0_ffn_b2")}
    arrays["x_t"] = np.ascontiguousarray(np.transpose(inputs["x"], (0, 2, 1)))
    arrays["ctx_t"] = np.ascontiguousarray(np.transpose(inputs["ctx_1024"], (0, 2, 1)))
    arrays["bq_cols"] = np.ascontiguousarray(np.reshape(inputs["L0_attn_bq"], (NG, P)).transpose(1, 0))
    arrays["b1_cols"] = np.ascontiguousarray(np.reshape(inputs["L0_ffn_b1"], (E, NF, P)).transpose(2, 0, 1))
    for short, name in (("wq_t", "L0_attn_Wq"), ("wk_t", "L0_attn_Wk"), ("wv_t", "L0_attn_Wv"),
                        ("wo_t", "L0_attn_Wo"), ("xwq_t", "L0_xattn_wq"), ("xwk_t", "L0_xattn_wk"),
                        ("xwv_t", "L0_xattn_wv"), ("xwo_t", "L0_xattn_wo")):
        arrays[short] = np.ascontiguousarray(np.transpose(inputs[name], (1, 0)))
    lane, f32 = np.arange(P), np.float32
    arrays["identity"] = np.eye(P, dtype=f32)
    arrays["same_head"] = (lane[:, None] // DH == lane[None, :] // DH).astype(f32)
    arrays["head_of"] = (lane[:, None] // DH == np.arange(HG)[None, :]).astype(f32)
    arrays["earlier"] = (lane[:, None] < lane[None, :]).astype(f32)
    arrays["ones"] = np.ones((P, P), f32)
    arrays["zeros"] = np.zeros((P, D), f32)
    arrays["expert_no"] = np.tile(np.arange(E, dtype=f32), (P, 1))
    arrays["expert_base"] = np.tile(np.arange(E, dtype=f32) * CAP, (P, 1))
    arrays["token_no"] = (np.arange(B * NT)[None, :] * P + lane[:, None] + 1).astype(f32)
    arrays["dump_slot"] = (SLOTS + lane[:, None]).astype(f32)
    arrays["empty_row"] = (NTOK + 1 + lane[:, None]).astype(f32)
    arrays["table_init"] = np.zeros((SLOTS + P, 2), f32)

    nc = _bacc.Bacc("TRN2", target_bir_lowering=False, num_devices=1)
    t, ins = {}, {}
    for name, a in arrays.items():
        t[name] = nc.dram_tensor(f"in_{name}", a.shape, mybir.dt.from_np(a.dtype), kind="ExternalInput").ap()
        ins[f"in_{name}"] = a
    t["out"] = nc.dram_tensor("out_0", (B, T, D), F32, kind="ExternalOutput").ap()
    program(nc, t)
    r = _run(nc, [ins], core_ids=[0])
    return r.results[0]["out_0"]
```
